# Optimizing a Trainium2 kernel written in Bass

```python
import numpy as np
import jax
import jax.numpy as jnp

def _softmax(x, axis=-1):
    return jax.nn.softmax(x, axis=axis)

def _gelu(x):
    return jax.nn.gelu(x, approximate=True)

def _silu(x):
    return jax.nn.silu(x)

def _sigmoid(x):
    return jax.nn.sigmoid(x)

def _layernorm(x, axis=-1, eps=1e-05):
    m = jnp.mean(x, axis=axis, keepdims=True)
    v = jnp.var(x, axis=axis, keepdims=True)
    return (x - m) / jnp.sqrt(v + eps)

def _scatter_add(tgt, idx, src, axis=0):
    return tgt.at[idx].add(src)

def _segment_sum(src, seg, n):
    return jax.ops.segment_sum(src, seg, n)
kernel_name = 'mk_seq_postln_d1_jaxref_r4_1a40e1'

def setup_inputs(seed: int=0):
    np.random.seed(seed)
    _w = jnp.asarray

    def _L0_attn_setup():
        import jax, jax.numpy as jnp
        import numpy as np
        import math
        B, N, E, D = (4, 2048, 256, 64)
        key = jax.random.key(seed)
        kx, kq, kk, kv, ko = jax.random.split(key, 5)
        x = jax.random.normal(kx, (B, N, E), dtype=jnp.float32)
        wq = jnp.sign(jax.random.normal(kq, (D, E), dtype=jnp.float32)) / math.sqrt(E)
        wk = jnp.sign(jax.random.normal(kk, (D, E), dtype=jnp.float32)) / math.sqrt(E)
        wv = jnp.sign(jax.random.normal(kv, (D, E), dtype=jnp.float32)) / math.sqrt(E)
        wo = jnp.sign(jax.random.normal(ko, (E, D), dtype=jnp.float32)) / math.sqrt(D)
        return {'x': x, 'wq': wq, 'wk': wk, 'wv': wv, 'wo': wo}
    _L0_attn_in = _L0_attn_setup()

    def _L0_ffn_setup():
        import jax, jax.numpy as jnp
        import numpy as np
        D_IN, D_HID = (256, 1024)

        def _ternary(key, shape):
            return jax.random.randint(key, shape, -1, 2).astype(jnp.float32)

        def _tlin(x, w, s):
            return jnp.einsum('bsi,oi->bso', x, w) * s
        key = jax.random.key(seed)
        ks = jax.random.split(key, 12)
        inv = lambda fan: 1.0 / np.sqrt(fan).astype(np.float32)
        return {'x': jax.random.normal(ks[0], (4, 512, D_IN), dtype=jnp.float32), 'w1_w': _ternary(ks[1], (D_HID, D_IN)), 'w1_s': jax.random.uniform(ks[2], (D_HID,), dtype=jnp.float32) * inv(D_IN), 'w2_w': _ternary(ks[3], (D_HID, D_IN)), 'w2_s': jax.random.uniform(ks[4], (D_HID,), dtype=jnp.float32) * inv(D_IN), 'h1_w': _ternary(ks[5], (D_HID, D_HID)), 'h1_s': jax.random.uniform(ks[6], (D_HID,), dtype=jnp.float32) * inv(D_HID), 'h2_w': _ternary(ks[7], (D_HID, D_HID)), 'h2_s': jax.random.uniform(ks[8], (D_HID,), dtype=jnp.float32) * inv(D_HID), 'w3_w': _ternary(ks[9], (D_IN, D_HID)), 'w3_s': jax.random.uniform(ks[10], (D_IN,), dtype=jnp.float32) * inv(D_HID)}
    _L0_ffn_in = _L0_ffn_setup()
    _d = {'L0_attn_x': _L0_attn_in['x'], 'L0_attn_wq': _L0_attn_in['wq'], 'L0_attn_wk': _L0_attn_in['wk'], 'L0_attn_wv': _L0_attn_in['wv'], 'L0_attn_wo': _L0_attn_in['wo'], 'L0_ffn_w1_w': _L0_ffn_in['w1_w'], 'L0_ffn_w1_s': _L0_ffn_in['w1_s'], 'L0_ffn_w2_w': _L0_ffn_in['w2_w'], 'L0_ffn_w2_s': _L0_ffn_in['w2_s'], 'L0_ffn_h1_w': _L0_ffn_in['h1_w'], 'L0_ffn_h1_s': _L0_ffn_in['h1_s'], 'L0_ffn_h2_w': _L0_ffn_in['h2_w'], 'L0_ffn_h2_s': _L0_ffn_in['h2_s'], 'L0_ffn_w3_w': _L0_ffn_in['w3_w'], 'L0_ffn_w3_s': _L0_ffn_in['w3_s']}
    _x0 = _d['L0_attn_x']
    _d['L0_attn_x'] = jax.random.normal(jax.random.fold_in(jax.random.key(seed), 1), (1, 4096, 256), dtype=_x0.dtype)
    del _x0
    return _d

def reference(L0_attn_x, L0_attn_wq, L0_attn_wk, L0_attn_wv, L0_attn_wo, L0_ffn_w1_w, L0_ffn_w1_s, L0_ffn_w2_w, L0_ffn_w2_s, L0_ffn_h1_w, L0_ffn_h1_s, L0_ffn_h2_w, L0_ffn_h2_s, L0_ffn_w3_w, L0_ffn_w3_s):

    def _L0_attn_ref(x, wq, wk, wv, wo):
        import jax, jax.numpy as jnp
        import numpy as np
        import math
        B, N, E, D = (4, 2048, 256, 64)
        Q = jnp.einsum('bne,de->bnd', x, wq)
        K = jnp.einsum('bne,de->bnd', x, wk)
        V = jnp.einsum('bne,de->bnd', x, wv)
        energy = jnp.einsum('bnd,bne->bde', K, V)
        context = jnp.einsum('bnd,bde->bne', Q, energy)
        context = context * jnp.asarray(math.sqrt(3.0 / D), dtype=context.dtype)
        out = jnp.einsum('bnd,ed->bne', context, wo)
        return out

    def _L0_ffn_ref(x, w1_w, w1_s, w2_w, w2_s, h1_w, h1_s, h2_w, h2_s, w3_w, w3_s):
        import jax, jax.numpy as jnp
        import numpy as np
        D_IN, D_HID = (256, 1024)

        def _ternary(key, shape):
            return jax.random.randint(key, shape, -1, 2).astype(jnp.float32)

        def _tlin(x, w, s):
            return jnp.einsum('bsi,oi->bso', x, w) * s
        h = jax.nn.silu(_tlin(x, w1_w, w1_s)) * _tlin(x, w2_w, w2_s)
        h = jax.nn.gelu(_tlin(h, h1_w, h1_s), approximate=False)
        h = jax.nn.gelu(_tlin(h, h2_w, h2_s), approximate=False)
        return _tlin(h, w3_w, w3_s)
    x = L0_attn_x
    x = _layernorm(x + _L0_attn_ref(x, L0_attn_wq, L0_attn_wk, L0_attn_wv, L0_attn_wo), axis=-1)
    x = _layernorm(x + _L0_ffn_ref(x, L0_ffn_w1_w, L0_ffn_w1_s, L0_ffn_w2_w, L0_ffn_w2_s, L0_ffn_h1_w, L0_ffn_h1_s, L0_ffn_h2_w, L0_ffn_h2_s, L0_ffn_w3_w, L0_ffn_w3_s), axis=-1)
    return x

_drawn_inputs = setup_inputs


def setup_inputs(seed=0):
    import zlib

    import numpy as np

    out = dict(_drawn_inputs(seed))
    spreads = {}
    factors = {'L0_ffn_w1_w': 8.0,
     'L0_ffn_w1_s': 8.0,
     'L0_ffn_w2_w': 8.0,
     'L0_ffn_w2_s': 8.0,
     'L0_ffn_h1_w': 8.0,
     'L0_ffn_h1_s': 8.0,
     'L0_ffn_h2_w': 8.0,
     'L0_ffn_h2_s': 8.0,
     'L0_ffn_w3_w': 8.0,
     'L0_ffn_w3_s': 8.0}
    for name, (base, spread) in spreads.items():
        noise = np.random.default_rng([zlib.crc32(name.encode()), seed]).standard_normal(out[name].shape)
        drawn = base * np.exp(spread * noise) if base else spread * noise
        out[name] = jnp.asarray(drawn.astype(out[name].dtype))
    for name, factor in factors.items():
        out[name] = (out[name] * factor).astype(out[name].dtype)
    return out
```

```python
import math

import concourse.bass as bass
from concourse import mybir
from contextlib import ExitStack

P = 128
TOK, E, D, HID = 4096, 256, 64, 1024
BLK = 512
NB = TOK // BLK
TPB = BLK // P
EC = E // P
HC = HID // P
EPS = 1e-5
CTX_SCALE = math.sqrt(3.0 / D)

W1_AT, W2_AT = 0, EC * HID
H1_AT = 2 * EC * HID
H2_AT = H1_AT + HC * HID
W3_AT = H2_AT + HC * HID
W_COLS = W3_AT + HC * E
WCH = 1024
NCH = W_COLS // WCH
CH_L1, CH_H1, CH_H2, CH_W3 = 4, 12, 20, 22
STAGES = 2

RING = 4
TILES = 4 * HC
NG = 3
SPLITS = 3 * HC
TR_AFTER = 5


def build(nc, xT_in, xr_in, wkv_in, wq_in, wo_in, w1_in, w2_in, h1_in, h2_in, w3_in, sc_in, s3_in, out):
    f32, f32r, i32 = mybir.dt.float32, mybir.dt.float32r, mybir.dt.int32
    ALU, ACT, AX = mybir.AluOpType, mybir.ActivationFunctionType, mybir.AxisListType

    ctx = ExitStack()
    with ctx:
        def sb(name, shape, dt=f32):
            return ctx.enter_context(nc.sbuf_tensor(name, shape, dt))

        def sem(name):
            return ctx.enter_context(nc.semaphore(name))

        W = sb("W", [P, W_COLS], f32r)
        hid = [sb(f"hid{i}", [P, 2, HC, BLK], f32r) for i in range(2)]
        x1T = sb("x1T", [P, 2, EC, BLK], f32r)
        xbuf = sb("xbuf", [P, 4, TPB * E])
        stage = sb("stage", [P, STAGES, WCH])
        sg = sb("sg", [P, 2, BLK])
        g = sb("g", [P, NG, BLK])
        scaled = sb("scaled", [P, TPB, E])
        M = sb("M", [P, EC, E])
        T1 = sb("T1", [D, E])
        ET = sb("ET", [D, D])
        wkv = sb("wkv", [P, EC, 2 * D])
        wq = sb("wq", [D, E])
        wo = sb("wo", [D, E])
        s3b = sb("s3b", [P, E])
        sc = sb("sc", [P, 4, HC])
        ident = sb("ident", [P, P])
        ones = sb("ones", [P, 1])
        nhalf = sb("nhalf", [P, TPB])
        eps = sb("eps", [P, TPB])
        st = [sb(f"st{i}", [P, TPB, 6]) for i in range(2)]
        mv = [sb(f"mv{i}", [P, TPB, 2]) for i in range(2)]
        ve = [sb(f"ve{i}", [P, TPB]) for i in range(2)]
        rstd = [sb(f"rstd{i}", [P, TPB]) for i in range(2)]
        lowf = sb("lowf", [P, 4])
        flag = sb("flag", [1, 4], i32)
        acc = ctx.enter_context(nc.psum_tensor("acc", [P, RING, BLK], f32))
        rows = ctx.enter_context(nc.psum_tensor("rows", [P, TPB, E], f32))
        trp = ctx.enter_context(nc.psum_tensor("trp", [P, EC, BLK], f32))
        kv = [scaled[:, 0:2, :].rearrange("p a e -> p (a e)"), scaled[:, 2:4, :].rearrange("p a e -> p (a e)")]

        cst_in = sem("cst_in")
        made = sem("made")
        xf_in = [sem(f"xf_in{i}") for i in range(4)]
        staged = [sem(f"staged{i}") for i in range(STAGES)]
        w_in = [sem(f"w_in{i}") for i in range(STAGES)]
        kv_ready, kv_out = sem("kv_ready"), sem("kv_out")
        et_ready, et_out = sem("et_ready"), sem("et_out")
        t1_ready, t1_out = sem("t1_ready"), sem("t1_out")
        m_ready, m_out = sem("m_ready"), sem("m_out")
        fold_done, lowf_done = sem("fold_done"), sem("lowf_done")
        flagsum, flag_done = sem("flagsum"), sem("flag_done")
        tile_ready = sem("tile_ready")
        silu_done = sem("silu_done")
        h_made = sem("h_made")
        hi_done = sem("hi_done")
        split_done = sem("split_done")
        op_ready, w3_ready, tr_ready = sem("op_ready"), sem("w3_ready"), sem("tr_ready")
        w3_used = sem("w3_used")
        trhi_done, trlo_done = sem("trhi_done"), sem("trlo_done")
        sum_done = [sem(f"sum_done{i}") for i in range(2)]
        stats_done = [sem(f"stats_done{i}") for i in range(2)]
        aggr_done = [sem(f"aggr_done{i}") for i in range(2)]
        ve_done = [sem(f"ve_done{i}") for i in range(2)]
        rstd_done = [sem(f"rstd_done{i}") for i in range(2)]
        norm_done = [sem(f"norm_done{i}") for i in range(2)]
        stored = sem("stored")

        weight_of = ([(w1_in, c) for c in range(EC)] + [(w2_in, c) for c in range(EC)]
                     + [(h1_in, k) for k in range(HC)] + [(h2_in, k) for k in range(HC)]
                     + [(w3_in, c) for c in range(HC * E // WCH)])

        def weights_landed(eng, chunks):
            for s in range(STAGES):
                eng.wait_ge(w_in[s], 16 * ((chunks - s + STAGES - 1) // STAGES))

        block = ctx.enter_context(nc.Block())

        @block.sync
        def _(sp):
            n = 0
            for dst, src in ((wkv[:, :, :], wkv_in), (wq[:, :], wq_in), (wo[:, :], wo_in), (sc[:, :, :], sc_in),
                             (s3b[:, :], s3_in.partition_broadcast(P))):
                sp.dma_start(dst, src).then_inc(cst_in, 16)
                n += 1

            def settle(i):
                sp.wait_ge(staged[i % STAGES], 16 * (i // STAGES + 1))
                sp.dma_start(W[:, i * WCH:(i + 1) * WCH].bitcast(f32), stage[:, i % STAGES, :]).then_inc(w_in[i % STAGES], 16)

            for i in range(NCH):
                if i >= STAGES:
                    sp.wait_ge(w_in[i % STAGES], 16 * (i // STAGES))
                src, c = weight_of[i]
                sp.dma_start(stage[:, i % STAGES, :], src[:, c * WCH:(c + 1) * WCH]).then_inc(staged[i % STAGES], 16)
                if i >= 1:
                    settle(i - 1)
            settle(NCH - 1)

            def turn(b, par, more):
                nxt = 1 - par
                if more:
                    sp.wait_ge(op_ready, b)
                    sp.dma_start(xbuf[:, nxt, :], xT_in[:, bass.ds((b + 1) * TPB * E, TPB * E)]).then_inc(xf_in[nxt], 16)
                sp.wait_ge(norm_done[1], b)
                sp.dma_start(out[:, bass.ds((b - 1) * TPB * E, TPB * E)], xbuf[:, 2 + nxt, :]).then_inc(stored, 16)
                if more:
                    sp.wait_ge(stored, b * 16)
                    sp.dma_start(xbuf[:, 2 + nxt, :], xr_in[:, bass.ds((b + 1) * TPB * E, TPB * E)]).then_inc(xf_in[2 + nxt], 16)

            with sp.Fori(0, (NB - 2) // 2) as i:
                turn(i * 2 + 1, 1, True)
                turn(i * 2 + 2, 0, True)
            turn(NB - 1, 1, False)
            turn(NB, 0, False)
            sp.wait_ge(stored, NB * 16)

        @block.gpsimd
        def _(pool):
            nc.gpsimd.memset(ident[:, :], 0.0).then_inc(made, 1)
            pool.wait_ge(made, 1)
            nc.gpsimd.affine_select(out=ident[:, :], in_=ident[:, :], compare_op=ALU.not_equal, fill=1.0, base=0,
                                    pattern=[[-1, P]], channel_multiplier=1).then_inc(made, 1)
            nc.gpsimd.memset(ones[:, :], 1.0).then_inc(made, 1)
            nc.gpsimd.memset(nhalf[:, :], -0.5).then_inc(made, 1)
            nc.gpsimd.memset(eps[:, :], EPS).then_inc(made, 1)
            pool.wait_ge(made, 5)

            def inverse_deviation(ln, n):
                pool.wait_ge(aggr_done[ln], n)
                nc.gpsimd.tensor_tensor(ve[ln][:, :], mv[ln][:, :, 1], eps[:, :], ALU.add).then_inc(ve_done[ln], 1)
                pool.wait_ge(ve_done[ln], n)
                nc.gpsimd.tensor_tensor(rstd[ln][:, :], ve[ln][:, :], nhalf[:, :], ALU.pow).then_inc(rstd_done[ln], 1)

            inverse_deviation(0, 1)
            inverse_deviation(0, 2)
            with pool.Fori(0, NB - 2) as i:
                inverse_deviation(1, i + 1)
                inverse_deviation(0, i + 3)
            inverse_deviation(1, NB - 1)
            inverse_deviation(1, NB)

        @block.scalar
        def _(act):
            for f in range(NB):
                if f >= 4:
                    act.wait_ge(kv_ready, f - 3)
                act.dma_start(xbuf[:, f % 4, :], xT_in[:, f * TPB * E:(f + 1) * TPB * E]).then_inc(xf_in[f % 4], 16)
            for b in range(2):
                act.wait_ge(kv_ready, 5 + b)
                act.dma_start(xbuf[:, b, :], xT_in[:, b * TPB * E:(b + 1) * TPB * E]).then_inc(xf_in[b], 16)
            for b in range(2):
                act.wait_ge(kv_ready, 7 + b)
                act.dma_start(xbuf[:, 2 + b, :], xr_in[:, b * TPB * E:(b + 1) * TPB * E]).then_inc(xf_in[2 + b], 16)

            def hi_of_transposed(b):
                act.wait_ge(tr_ready, b + 1)
                for c in range(EC):
                    nc.scalar.copy(x1T[:, 0, c, :], trp[:, c, :]).then_inc(trhi_done, 1)

            def gated(b, par):
                dst = hid[par]
                for j in range(HC + 1):
                    if j < HC:
                        act.wait_ge(tile_ready, b * TILES + (2 * j + 1))
                        if j >= 2:
                            act.wait_ge(h_made, b * HC + (j - 1))
                        nc.scalar.activation(sg[:, j % 2, :], acc[:, (2 * j) % RING, :], ACT.Silu,
                                             scale=sc[:, 0, j:j + 1]).then_inc(silu_done, 1)
                    if j >= 1:
                        act.wait_ge(h_made, b * HC + j)
                        nc.scalar.copy(dst[:, 0, j - 1, :], g[:, (j - 1) % NG, :]).then_inc(hi_done, 1)

            def hidden(b, layer, dst, between=None):
                for j in range(HC):
                    n = layer * HC + j
                    t = (layer + 1) * HC + j
                    act.wait_ge(tile_ready, b * TILES + (t + 1))
                    act.wait_ge(split_done, b * SPLITS + (n - NG + 1))
                    src = acc[:, t % RING, :]
                    nc.scalar.activation(g[:, n % NG, :], src, ACT.Gelu, scale=sc[:, 1 + layer, j:j + 1])
                    nc.scalar.activation(dst[:, 0, j, :], src, ACT.Gelu, scale=sc[:, 1 + layer, j:j + 1]).then_inc(hi_done, 1)
                    if between and j == TR_AFTER + 1:
                        between()

            def turn(b, par, more):
                gated(b, par)
                hidden(b, 1, hid[1 - par])
                hidden(b, 2, hid[par], (lambda: hi_of_transposed(b + 1)) if more else None)

            act.wait_ge(cst_in, 16 * 5)
            hi_of_transposed(0)
            turn(0, 0, True)
            with act.Fori(0, (NB - 2) // 2) as i:
                turn(i * 2 + 1, 1, True)
                turn(i * 2 + 2, 0, True)
            turn(NB - 1, 1, False)

        @block.vector
        def _(dve):
            bits = scaled[:, :, :].rearrange("p t e -> p (t e)").bitcast(i32)
            folds = [0]

            def folded(instruction):
                folds[0] += 1
                instruction.then_inc(fold_done, 1)
                dve.wait_ge(fold_done, folds[0])

            def weight_flag(s, first_chunk, chunks):
                weights_landed(dve, chunks)
                w = [W[:, i * WCH:(i + 1) * WCH].bitcast(i32) for i in range(first_chunk, chunks)]
                folded(nc.vector.tensor_tensor(bits, w[0], w[1], ALU.bitwise_or))
                for chunk in w[2:]:
                    folded(nc.vector.tensor_tensor(bits, bits, chunk, ALU.bitwise_or))
                folded(nc.vector.tensor_scalar(bits, bits, 0xFFF, None, ALU.bitwise_and))
                nc.vector.tensor_reduce(lowf[:, s:s + 1], bits, AX.X, ALU.max).then_inc(lowf_done, 1)

            def flag_out(s):
                dve.wait_ge(flagsum, s + 1)
                nc.vector.tensor_scalar(flag[:, s:s + 1], trp[0:1, 0, s:s + 1], 0.0, None, ALU.is_gt).then_inc(flag_done, 1)

            for f in range(NB):
                dve.wait_ge(kv_ready, f + 1)
                if f >= 2:
                    dve.wait_ge(et_ready, f - 1)
                nc.vector.tensor_copy(kv[f % 2], acc[:, f % 2, :]).then_inc(kv_out, 1)
            dve.wait_ge(et_ready, NB)
            nc.vector.tensor_copy(ET[:, :], acc[0:D, 2, 0:D]).then_inc(et_out, 1)
            dve.wait_ge(t1_ready, 1)
            nc.vector.tensor_scalar(T1[:, :], acc[0:D, 3, 0:E], CTX_SCALE, None, ALU.mult).then_inc(t1_out, 1)
            dve.wait_ge(m_ready, 1)
            nc.vector.tensor_copy(M[:, :, :], rows[:, 0:4:2, :]).then_inc(m_out, 1)

            def stats(ln, n, par):
                y = xbuf[:, 2 + par, :].rearrange("p (t e) -> p t e", e=E)
                dve.wait_ge(sum_done[ln], n)
                for q in range(TPB):
                    last = nc.vector.bn_stats(st[ln][:, q, :], y[:, q, :])
                last.then_inc(stats_done[ln], 1)
                dve.wait_ge(cst_in, 16 * 5)
                dve.wait_ge(stats_done[ln], n)
                for q in range(TPB):
                    last = nc.vector.bn_aggr(mv[ln][:, q, :], st[ln][:, q, :])
                last.then_inc(aggr_done[ln], 1)

            def normalise(ln, n, par):
                y = xbuf[:, 2 + par, :].rearrange("p (t e) -> p t e", e=E)
                dve.wait_ge(rstd_done[ln], n)
                for q in range(TPB):
                    last = nc.vector.tensor_scalar(y[:, q, :], y[:, q, :], mv[ln][:, q, 0:1], rstd[ln][:, q:q + 1],
                                                   ALU.subtract, ALU.mult)
                last.then_inc(norm_done[ln], 1)

            def residual1(b, par, loads):
                dve.wait_ge(op_ready, b + 1)
                dve.wait_ge(xf_in[2 + par], loads * 16)
                nc.vector.tensor_tensor(xbuf[:, 2 + par, :], rows[:, :, :].rearrange("p t e -> p (t e)"),
                                        xbuf[:, 2 + par, :], ALU.add).then_inc(sum_done[0], 1)

            def residual2(b, par):
                dve.wait_ge(w3_ready, b + 1)
                nc.vector.tensor_tensor(scaled[:, :, :], rows[:, :, :],
                                        s3b[:, :].unsqueeze(1).broadcast_to([P, TPB, E]), ALU.mult).then_inc(w3_used, 1)
                dve.wait_ge(w3_used, b + 1)
                nc.vector.tensor_tensor(xbuf[:, 2 + par, :], scaled[:, :, :].rearrange("p t e -> p (t e)"),
                                        xbuf[:, 2 + par, :], ALU.add).then_inc(sum_done[1], 1)

            def lo_of_transposed(b):
                for c in range(EC):
                    dve.wait_ge(trhi_done, b * EC + (c + 1))
                    nc.vector.tensor_tensor(x1T[:, 1, c, :], trp[:, c, :], x1T[:, 0, c, :].bitcast(f32),
                                            ALU.subtract).then_inc(trlo_done, 1)

            def lo_part(b, n, dst, j):
                dve.wait_ge(hi_done, b * SPLITS + (n + 1))
                nc.vector.tensor_tensor(dst[:, 1, j, :], g[:, n % NG, :], dst[:, 0, j, :].bitcast(f32),
                                        ALU.subtract).then_inc(split_done, 1)

            def gated(b, par, first):
                for j in range(HC + 1):
                    if j < HC:
                        dve.wait_ge(silu_done, b * HC + (j + 1))
                        dve.wait_ge(tile_ready, b * TILES + (2 * j + 2))
                        if j >= NG or not first:
                            dve.wait_ge(split_done, b * SPLITS + (j - NG + 1))
                        nc.vector.scalar_tensor_tensor(g[:, j % NG, :], acc[:, (2 * j + 1) % RING, :], sc[:, 1, j:j + 1],
                                                       sg[:, j % 2, :], ALU.mult, ALU.mult).then_inc(h_made, 1)
                    if j >= 1:
                        lo_part(b, j - 1, hid[par], j - 1)

            def turn(b, par, loads, more, first=False, before=True):
                nxt = 1 - par
                if first:
                    weight_flag(1, CH_L1, CH_H1)
                gated(b, par, first)
                if first:
                    flag_out(1)
                    weight_flag(2, CH_H1, CH_H2)
                if before:
                    residual2(b - 1, nxt)
                    stats(1, b, nxt)
                for j in range(HC):
                    lo_part(b, HC + j, hid[nxt], j)
                    if j == 0 and before:
                        normalise(1, b, nxt)
                if first:
                    flag_out(2)
                    weight_flag(3, CH_H2, CH_W3)
                if more:
                    residual1(b + 1, nxt, loads)
                    stats(0, b + 2, nxt)
                for j in range(HC):
                    lo_part(b, 2 * HC + j, hid[par], j)
                    if j == 0 and more:
                        normalise(0, b + 2, nxt)
                    if j == TR_AFTER + 1 and more:
                        lo_of_transposed(b + 1)
                if first:
                    flag_out(3)

            dve.wait_ge(cst_in, 16 * 5)
            residual1(0, 0, 2 + 1)
            stats(0, 1, 0)
            weight_flag(0, 0, CH_L1)
            normalise(0, 1, 0)
            lo_of_transposed(0)
            flag_out(0)
            turn(0, 0, 2 + 1, True, first=True, before=False)
            with dve.Fori(0, (NB - 2) // 2) as i:
                turn(i * 2 + 1, 1, i + 4, True)
                turn(i * 2 + 2, 0, i + 4, True)
            turn(NB - 1, 1, 0, False)
            residual2(NB - 1, 1)
            stats(1, NB, 1)
            normalise(1, NB, 1)

        @block.tensor
        def _(pe):
            def kv_products(f):
                pe.wait_ge(xf_in[f % 4], 16 * (f // 4 + 1))
                if f >= 2:
                    pe.wait_ge(kv_out, f - 1)
                xt = xbuf[:, f % 4, :].rearrange("p (c t n) -> p c t n", c=EC, t=TPB)
                for q in range(TPB):
                    for c in range(EC):
                        last = nc.tensor.matmul(acc[:, f % 2, q * P:(q + 1) * P], xt[:, c, q, :], wkv[:, c, :],
                                                start=c == 0, stop=c == EC - 1)
                last.then_inc(kv_ready, 1)

            def energy(f):
                pe.wait_ge(kv_out, f + 1)
                for q in range(TPB):
                    k, v = kv[f % 2][:, q * P:q * P + D], kv[f % 2][:, q * P + D:(q + 1) * P]
                    last = nc.tensor.matmul(acc[0:D, 2, 0:D], v, k, start=(f == 0 and q == 0),
                                            stop=(f == NB - 1 and q == TPB - 1))
                last.then_inc(et_ready, 1)

            pe.wait_ge(cst_in, 16 * 5)
            kv_products(0)
            for f in range(NB):
                if f + 1 < NB:
                    kv_products(f + 1)
                energy(f)
            pe.wait_ge(et_out, 1)
            nc.tensor.matmul(acc[0:D, 3, 0:E], ET[:, :], wo[:, :], start=True, stop=True).then_inc(t1_ready, 1)
            pe.wait_ge(t1_out, 1)
            for c in range(EC):
                last = nc.tensor.matmul(rows[:, 2 * c, :], wq[:, c * P:(c + 1) * P], T1[:, :], start=True, stop=True)
            last.then_inc(m_ready, 1)
            pe.wait_ge(m_out, 1)

            def attention_out(b, par, loads):
                pe.wait_ge(xf_in[par], loads * 16)
                xt = xbuf[:, par, :].rearrange("p (c t n) -> p c t n", c=EC, t=TPB)
                for q in range(TPB):
                    for c in range(EC):
                        last = nc.tensor.matmul(rows[:, q, :], xt[:, c, q, :], M[:, c, :], start=c == 0, stop=c == EC - 1)
                last.then_inc(op_ready, 1)

            def transposes(b, par):
                pe.wait_ge(norm_done[0], b + 1)
                y = xbuf[:, 2 + par, :].rearrange("p (t e) -> p t e", e=E)
                for c in range(EC):
                    for q in range(TPB):
                        last = nc.tensor.transpose(trp[:, c, q * P:(q + 1) * P], y[:, q, c * P:(c + 1) * P], ident[:, :])
                last.then_inc(tr_ready, 1)

            def flag_sum(s):
                pe.wait_ge(lowf_done, s + 1)
                nc.tensor.matmul(trp[0:1, 0, s:s + 1], lowf[:, s:s + 1], ones[:, :], start=True, stop=True).then_inc(flagsum, 1)

            inexact = [None] * 4

            def load_flag(s):
                pe.wait_ge(flag_done, s + 1)
                inexact[s] = pe.value_load(flag[0:1, s:s + 1], min_val=0, max_val=1)

            def either(s, stage_of):
                with pe.If(inexact[s] == 0):
                    stage_of(lambda ap: ap)
                with pe.Else():
                    stage_of(lambda ap: ap.bitcast(f32))

            def tile_free(b, t, after_previous):
                u = t - RING
                if u < 0:
                    if after_previous:
                        pe.wait_ge(hi_done, (b - 1) * SPLITS + (u + TILES - HC + 1))
                elif u < 2 * HC:
                    pe.wait_ge(silu_done if u % 2 == 0 else h_made, b * HC + (u // 2 + 1))
                else:
                    pe.wait_ge(hi_done, b * SPLITS + (u - HC + 1))

            def stage_l1(b, par, view, after_previous):
                for t in range(2 * HC):
                    j, at = t // 2, (W1_AT, W2_AT)[t % 2]
                    tile_free(b, t, after_previous)
                    for c in range(EC):
                        w = view(W[:, at + c * HID + j * P:at + c * HID + (j + 1) * P])
                        for part in range(2):
                            last = nc.tensor.matmul(acc[:, t % RING, :], w, view(x1T[:, part, c, :]),
                                                    start=c == 0 and part == 0, stop=c == EC - 1 and part == 1)
                    last.then_inc(tile_ready, 1)

            def stage_hidden(b, layer, src, view, js, between=None):
                at = (H1_AT, H2_AT)[layer - 1]
                for j in js:
                    t = (layer + 1) * HC + j
                    tile_free(b, t, True)
                    for k in range(HC):
                        if j == 0:
                            pe.wait_ge(split_done, b * SPLITS + ((layer - 1) * HC + k + 1))
                        w = view(W[:, at + k * HID + j * P:at + k * HID + (j + 1) * P])
                        for part in range(2):
                            last = nc.tensor.matmul(acc[:, t % RING, :], w, view(src[:, part, k, :]),
                                                    start=k == 0 and part == 0, stop=k == HC - 1 and part == 1)
                    last.then_inc(tile_ready, 1)

            def stage_w3(b, src, view):
                for q0 in range(TPB // 2):
                    for k in range(HC):
                        if q0 == 0:
                            pe.wait_ge(split_done, b * SPLITS + (2 * HC + k + 1))
                        w = view(W[:, W3_AT + k * E:W3_AT + (k + 1) * E])
                        for q in (q0, q0 + 2):
                            for part in range(2):
                                last = nc.tensor.matmul(rows[:, q, :], view(src[:, part, k, q * P:(q + 1) * P]), w,
                                                        start=k == 0 and part == 0, stop=k == HC - 1 and part == 1)
                last.then_inc(w3_ready, 1)

            def down(b, par, after_op):
                if after_op:
                    pe.wait_ge(sum_done[0], b + 2)
                either(3, lambda view: stage_w3(b, hid[par], view))

            def turn(b, par, loads, more, first=False, before=True):
                nxt = 1 - par
                pe.wait_ge(trlo_done, (b + 1) * EC)
                either(0, lambda view: stage_l1(b, par, view, not first))
                if first:
                    flag_sum(1)
                    load_flag(1)
                    weights_landed(pe, CH_H1)
                if before:
                    down(b - 1, nxt, True)
                either(1, lambda view: stage_hidden(b, 1, hid[par], view, range(HC)))
                if more:
                    if before:
                        pe.wait_ge(w3_used, b)
                    attention_out(b + 1, nxt, loads)
                if first:
                    flag_sum(2)
                    load_flag(2)
                    weights_landed(pe, CH_H2)
                cut = TR_AFTER + 1
                either(2, lambda view: stage_hidden(b, 2, hid[nxt], view, range(cut)))
                if more:
                    transposes(b + 1, nxt)
                either(2, lambda view: stage_hidden(b, 2, hid[nxt], view, range(cut, HC)))
                if first:
                    pe.wait_ge(trlo_done, (b + 2) * EC)
                    flag_sum(3)
                    load_flag(3)
                    weights_landed(pe, CH_W3)

            pe.wait_ge(made, 5)
            attention_out(0, 0, 2 + 1)
            transposes(0, 0)
            pe.wait_ge(trlo_done, EC)
            flag_sum(0)
            load_flag(0)
            weights_landed(pe, CH_L1)
            turn(0, 0, 2 + 1, True, first=True, before=False)
            with pe.Fori(0, (NB - 2) // 2) as i:
                turn(i * 2 + 1, 1, i + 4, True)
                turn(i * 2 + 2, 0, i + 4, True)
            turn(NB - 1, 1, 0, False)
            pe.wait_ge(w3_used, NB - 1)
            down(NB - 1, 1, False)


def kernel(**inputs):
    import numpy as np
    import concourse.bacc as bacc
    from concourse.bass_utils import run_bass_kernel_spmd

    def get(name):
        return np.asarray(inputs["L0_" + name])

    x = get("attn_x").reshape(P, NB, TPB, E)
    arrays = {
        "xT": x.reshape(P, NB, TPB, EC, P).transpose(4, 1, 3, 2, 0).reshape(P, TOK * EC),
        "x_rows": x.reshape(P, NB * TPB * E),
        "wkv": np.concatenate([get("attn_wk"), get("attn_wv")], 0).T.reshape(EC, P, 2 * D).transpose(1, 0, 2),
        "wq": get("attn_wq"),
        "woT": get("attn_wo").T,
        "w1T": get("ffn_w1_w").T.reshape(EC, P, HID).transpose(1, 0, 2).reshape(P, EC * HID),
        "w2T": get("ffn_w2_w").T.reshape(EC, P, HID).transpose(1, 0, 2).reshape(P, EC * HID),
        "h1T": get("ffn_h1_w").T.reshape(HC, P, HID).transpose(1, 0, 2).reshape(P, HC * HID),
        "h2T": get("ffn_h2_w").T.reshape(HC, P, HID).transpose(1, 0, 2).reshape(P, HC * HID),
        "w3T": get("ffn_w3_w").T.reshape(HC, P, E).transpose(1, 0, 2).reshape(P, HC * E),
        "scales": np.stack([get("ffn_" + n).reshape(HC, P) for n in ("w1_s", "w2_s", "h1_s", "h2_s")]).transpose(2, 0, 1),
        "s3": get("ffn_w3_s"),
    }
    arrays = {n: np.ascontiguousarray(a) for n, a in arrays.items()}
    nc = bacc.Bacc("TRN2", target_bir_lowering=False, num_devices=1)
    args = [nc.dram_tensor("in_" + n, a.shape, mybir.dt.from_np(a.dtype), kind="ExternalInput").ap() for n, a in arrays.items()]
    out = nc.dram_tensor("out", (P, NB * TPB * E), mybir.dt.float32, kind="ExternalOutput").ap()
    build(nc, *args, out)
    r = run_bass_kernel_spmd(nc, [{"in_" + n: a for n, a in arrays.items()}], core_ids=[0])
    return r.results[0]["out"].reshape(1, TOK, E)
```

```python
import math

import concourse.bass as bass
from concourse import mybir
from contextlib import ExitStack

P = 128
TOK, E, D, HID = 4096, 256, 64, 1024
BLK = 512
NB = TOK // BLK
NCST = 4
TPB = BLK // P
EC = E // P
HC = HID // P
EPS = 1e-5
CTX_SCALE = math.sqrt(3.0 / D)

W1_AT, W2_AT = 0, EC * HID
H1_AT = 2 * EC * HID
H2_AT = H1_AT + HC * HID
W3_AT = H2_AT + HC * HID
W_COLS = W3_AT + HC * E
WCH = 1024
NCH = W_COLS // WCH
CH_L1, CH_H1, CH_H2, CH_W3 = 4, 12, 20, 22
EARLY = CH_H1
STAGES = 8
LATE = 2

RING = 4
TILES = 4 * HC
NG = 3
SPLITS = 3 * HC
FLAG2_AFTER = 6
TR_AFTER = 5


def build(nc, xT_in, xr_in, wkv_src, wq_in, wo_in, w1_in, w2_in, h1_in, h2_in, w3_in, sc_in, s3_in, out):
    f32, f32r, i32 = mybir.dt.float32, mybir.dt.float32r, mybir.dt.int32
    ALU, ACT, AX = mybir.AluOpType, mybir.ActivationFunctionType, mybir.AxisListType

    ctx = ExitStack()
    with ctx:
        def sb(name, shape, dt=f32):
            return ctx.enter_context(nc.sbuf_tensor(name, shape, dt))

        def sem(name):
            return ctx.enter_context(nc.semaphore(name))

        W = sb("W", [P, W_COLS], f32r)
        with nc.sbuf_tensor("stage", [P, STAGES, WCH], f32) as stage:
            pass
        hid = [None, sb("hid1", [P, 2, HC, BLK], f32r)]
        hid[0] = sb("hid0", [P, 2, HC, BLK], f32r)
        x1T = sb("x1T", [P, 2, EC, BLK], f32r)
        xbuf = sb("xbuf", [P, 4, TPB * E])
        late = sb("late", [P, LATE, WCH])
        sg = sb("sg", [P, 2, BLK])
        g = sb("g", [P, NG, BLK])
        scaled = sb("scaled", [P, TPB, E])
        M = sb("M", [P, EC, E])
        T1 = sb("T1", [D, E])
        ET = sb("ET", [D, D])
        wkv = sb("wkv", [P, EC, 2 * D])
        wq = sb("wq", [D, E])
        wo = sb("wo", [D, E])
        s3b = sb("s3b", [P, E])
        sc = sb("sc", [P, 4, HC])
        ident = sb("ident", [P, P])
        ones = sb("ones", [P, 1])
        nhalf = sb("nhalf", [P, TPB])
        eps = sb("eps", [P, TPB])
        st = [sb(f"st{i}", [P, TPB, 6]) for i in range(2)]
        mv = [sb(f"mv{i}", [P, TPB, 2]) for i in range(2)]
        ve = [sb(f"ve{i}", [P, TPB]) for i in range(2)]
        rstd = [sb(f"rstd{i}", [P, TPB]) for i in range(2)]
        lowf = sb("lowf", [P, 4])
        flag = sb("flag", [1, 4], i32)
        acc = ctx.enter_context(nc.psum_tensor("acc", [P, RING, BLK], f32))
        rows = ctx.enter_context(nc.psum_tensor("rows", [P, TPB, E], f32))
        trp = ctx.enter_context(nc.psum_tensor("trp", [P, EC, BLK], f32))
        kv = [scaled[:, 0:2, :].rearrange("p a e -> p (a e)"), scaled[:, 2:4, :].rearrange("p a e -> p (a e)")]

        wkv_in = sem("wkv_in")
        cst_in = sem("cst_in")
        made = sem("made")
        xf_in = [sem(f"xf_in{i}") for i in range(4)]
        staged = [sem(f"staged{i}") for i in range(STAGES)]
        staged_late = [sem(f"staged_late{i}") for i in range(LATE)]
        w_in = [sem(f"w_in{i}") for i in range(STAGES)]
        w_in_late = [sem(f"w_in_late{i}") for i in range(LATE)]
        kv_ready, kv_out = sem("kv_ready"), sem("kv_out")
        et_ready, et_out = sem("et_ready"), sem("et_out")
        t1_ready, t1_out = sem("t1_ready"), sem("t1_out")
        m_ready, m_out = sem("m_ready"), sem("m_out")
        fold_done, lowf_done = sem("fold_done"), sem("lowf_done")
        flagsum, flag_done = sem("flagsum"), sem("flag_done")
        tile_ready = sem("tile_ready")
        silu_done = sem("silu_done")
        h_made = sem("h_made")
        hi_done = sem("hi_done")
        split_done = sem("split_done")
        op_ready, w3_ready, tr_ready = sem("op_ready"), sem("w3_ready"), sem("tr_ready")
        w3_used = sem("w3_used")
        trhi_done, trlo_done = sem("trhi_done"), sem("trlo_done")
        sum_done = [sem(f"sum_done{i}") for i in range(2)]
        stats_done = [sem(f"stats_done{i}") for i in range(2)]
        aggr_done = [sem(f"aggr_done{i}") for i in range(2)]
        ve_done = [sem(f"ve_done{i}") for i in range(2)]
        rstd_done = [sem(f"rstd_done{i}") for i in range(2)]
        norm_done = [sem(f"norm_done{i}") for i in range(2)]
        stored = sem("stored")
        last_hi_done = sem("last_hi_done")
        tail_scaled, tail_sum, tail_stats, tail_aggr = sem("tail_scaled"), sem("tail_sum"), sem("tail_stats"), sem("tail_aggr")
        tail_ve, tail_rstd_done, tail_done = sem("tail_ve"), sem("tail_rstd_done"), sem("tail_done")

        weight_of = ([(w1_in, c) for c in range(EC)] + [(w2_in, c) for c in range(EC)]
                     + [(h1_in, k) for k in range(HC)] + [(h2_in, k) for k in range(HC)]
                     + [(w3_in, c) for c in range(HC * E // WCH)])

        def slot_of(i):
            if i < EARLY:
                k = i % STAGES
                return stage[:, k, :], i // STAGES, staged[k], w_in[k]
            k = (i - EARLY) % LATE
            return late[:, k, :], (i - EARLY) // LATE, staged_late[k], w_in_late[k]

        def chunk_landed(eng, i):
            _, before, _, landed = slot_of(i)
            eng.wait_ge(landed, 16 * (before + 1))

        block = ctx.enter_context(nc.Block())

        @block.sync
        def _(sp):
            sp.dma_start(wkv[:, :, :], wkv_src).then_inc(wkv_in, 16)

            def load(i):
                slot, before, arrived, landed = slot_of(i)
                if before:
                    sp.wait_ge(landed, 16 * before)
                src, c = weight_of[i]
                sp.dma_start(slot, src[:, c * WCH:(c + 1) * WCH]).then_inc(arrived, 16)

            def settle(i):
                slot, before, arrived, landed = slot_of(i)
                sp.wait_ge(arrived, 16 * (before + 1))
                sp.dma_start(W[:, i * WCH:(i + 1) * WCH].bitcast(f32), slot).then_inc(landed, 16)

            sp.wait_ge(xf_in[3], 16)
            load(0)
            load(1)
            for dst, src in ((wo[:, :], wo_in), (wq[:, :], wq_in), (sc[:, :, :], sc_in), (s3b[:, :], s3_in.partition_broadcast(P))):
                sp.dma_start(dst, src).then_inc(cst_in, 16)
            sp.wait_ge(xf_in[1], 16 * 2)
            settle(0)
            load(2)
            sp.wait_ge(xf_in[3], 16 * 2)
            load(3)
            for i in range(1, CH_L1):
                settle(i)
            for i in range(CH_L1, STAGES):
                load(i)
            for i in range(CH_L1, NCH):
                settle(i)
                ahead = CH_L1 if i < EARLY - CH_L1 else LATE
                if i == EARLY - CH_L1:
                    load(EARLY)
                    load(EARLY + 1)
                elif i + ahead < NCH and not EARLY - CH_L1 < i < EARLY:
                    load(i + ahead)

            def turn(b, par, more):
                nxt = 1 - par
                if more:
                    sp.wait_ge(op_ready, b)
                    sp.dma_start(xbuf[:, nxt, :], xT_in[:, bass.ds((b + 1) * TPB * E, TPB * E)]).then_inc(xf_in[nxt], 16)
                sp.wait_ge(norm_done[1], b)
                sp.dma_start(out[:, bass.ds((b - 1) * TPB * E, TPB * E)], xbuf[:, 2 + nxt, :]).then_inc(stored, 16)
                if more:
                    sp.wait_ge(stored, b * 16)
                    sp.dma_start(xbuf[:, 2 + nxt, :], xr_in[:, bass.ds((b + 1) * TPB * E, TPB * E)]).then_inc(xf_in[2 + nxt], 16)

            with sp.Fori(0, (NB - 2) // 2) as i:
                turn(i * 2 + 1, 1, True)
                turn(i * 2 + 2, 0, True)
            turn(NB - 1, 1, False)
            for q in range(TPB):
                sp.wait_ge(tail_done, q + 1)
                at = (NB - 1) * TPB * E + q * E
                sp.dma_start(out[:, at:at + E], xbuf[:, 3, q * E:(q + 1) * E]).then_inc(stored, 16)
            sp.wait_ge(stored, (NB - 1 + TPB) * 16)

        @block.gpsimd
        def _(pool):
            nc.gpsimd.memset(ident[:, :], 0.0).then_inc(made, 1)
            pool.wait_ge(made, 1)
            nc.gpsimd.affine_select(out=ident[:, :], in_=ident[:, :], compare_op=ALU.not_equal, fill=1.0, base=0,
                                    pattern=[[-1, P]], channel_multiplier=1).then_inc(made, 1)
            nc.gpsimd.memset(ones[:, :], 1.0).then_inc(made, 1)
            nc.gpsimd.memset(nhalf[:, :], -0.5).then_inc(made, 1)
            nc.gpsimd.memset(eps[:, :], EPS).then_inc(made, 1)
            pool.wait_ge(made, 5)

            def inverse_deviation(ln, n):
                pool.wait_ge(aggr_done[ln], n)
                nc.gpsimd.tensor_tensor(ve[ln][:, :], mv[ln][:, :, 1], eps[:, :], ALU.add).then_inc(ve_done[ln], 1)
                pool.wait_ge(ve_done[ln], n)
                nc.gpsimd.tensor_tensor(rstd[ln][:, :], ve[ln][:, :], nhalf[:, :], ALU.pow).then_inc(rstd_done[ln], 1)

            inverse_deviation(0, 1)
            for j in range(HC):
                pool.wait_ge(hi_done, j + 1)
                nc.gpsimd.tensor_tensor(hid[0][:, 1, j, :], g[:, j % NG, :], hid[0][:, 0, j, :].bitcast(f32),
                                        ALU.subtract).then_inc(split_done, 1)
            inverse_deviation(0, 2)
            with pool.Fori(0, NB - 2) as i:
                inverse_deviation(1, i + 1)
                inverse_deviation(0, i + 3)
            inverse_deviation(1, NB - 1)
            for q in range(TPB):
                pool.wait_ge(tail_aggr, q + 1)
                nc.gpsimd.tensor_tensor(ve[1][:, q:q + 1], mv[1][:, q, 1:2], eps[:, 0:1], ALU.add).then_inc(tail_ve, 1)
                pool.wait_ge(tail_ve, q + 1)
                nc.gpsimd.tensor_tensor(rstd[1][:, q:q + 1], ve[1][:, q:q + 1], nhalf[:, 0:1], ALU.pow).then_inc(tail_rstd_done, 1)

        @block.scalar
        def _(act):
            for f in range(NB):
                if f >= 4:
                    act.wait_ge(kv_ready, f - 3)
                act.dma_start(xbuf[:, f % 4, :], xT_in[:, f * TPB * E:(f + 1) * TPB * E]).then_inc(xf_in[f % 4], 16)
            for b in range(2):
                act.wait_ge(kv_ready, 5 + b)
                act.dma_start(xbuf[:, b, :], xT_in[:, b * TPB * E:(b + 1) * TPB * E]).then_inc(xf_in[b], 16)
            for b in range(2):
                act.wait_ge(kv_ready, 7 + b)
                act.dma_start(xbuf[:, 2 + b, :], xr_in[:, b * TPB * E:(b + 1) * TPB * E]).then_inc(xf_in[2 + b], 16)

            def hi_of_transposed(b):
                act.wait_ge(tr_ready, b + 1)
                for c in range(EC):
                    nc.scalar.copy(x1T[:, 0, c, :], trp[:, c, :]).then_inc(trhi_done, 1)

            def gated(b, par):
                dst = hid[par]
                for j in range(HC + 1):
                    if j < HC:
                        act.wait_ge(tile_ready, b * TILES + (2 * j + 1))
                        if j >= 2:
                            act.wait_ge(h_made, b * HC + (j - 1))
                        nc.scalar.activation(sg[:, j % 2, :], acc[:, (2 * j) % RING, :], ACT.Silu,
                                             scale=sc[:, 0, j:j + 1]).then_inc(silu_done, 1)
                    if j >= 1:
                        act.wait_ge(h_made, b * HC + j)
                        nc.scalar.copy(dst[:, 0, j - 1, :], g[:, (j - 1) % NG, :]).then_inc(hi_done, 1)

            def hidden(b, layer, dst, between=None):
                for j in range(HC):
                    n = layer * HC + j
                    t = (layer + 1) * HC + j
                    act.wait_ge(tile_ready, b * TILES + (t + 1))
                    act.wait_ge(split_done, b * SPLITS + (n - NG + 1))
                    src = acc[:, t % RING, :]
                    whole = nc.scalar.activation(g[:, n % NG, :], src, ACT.Gelu, scale=sc[:, 1 + layer, j:j + 1])
                    if n == SPLITS - 1:
                        whole.then_inc(hi_done, 1)
                    else:
                        nc.scalar.activation(dst[:, 0, j, :], src, ACT.Gelu, scale=sc[:, 1 + layer, j:j + 1]).then_inc(hi_done, 1)
                    if between and j == TR_AFTER + 1:
                        between()

            def turn(b, par, more):
                gated(b, par)
                hidden(b, 1, hid[1 - par])
                hidden(b, 2, hid[par], (lambda: hi_of_transposed(b + 1)) if more else None)

            act.wait_ge(made, 5)
            nc.scalar.activation(sg[:, 0, 0:1], ones[:, :], ACT.Silu)
            act.wait_ge(cst_in, 16 * NCST)
            hi_of_transposed(0)
            turn(0, 0, True)
            with act.Fori(0, (NB - 2) // 2) as i:
                turn(i * 2 + 1, 1, True)
                turn(i * 2 + 2, 0, True)
            turn(NB - 1, 1, False)

        @block.vector
        def _(dve):
            bits = scaled[:, :, :].rearrange("p t e -> p (t e)").bitcast(i32)
            folds = [0]

            def folded(instruction):
                folds[0] += 1
                instruction.then_inc(fold_done, 1)
                dve.wait_ge(fold_done, folds[0])

            def fold(first, i):
                if i > first:
                    chunk_landed(dve, i - 1)
                    chunk_landed(dve, i)
                    w = [W[:, k * WCH:(k + 1) * WCH].bitcast(i32) for k in (i - 1, i)]
                    folded(nc.vector.tensor_tensor(bits, w[0] if i == first + 1 else bits, w[1], ALU.bitwise_or))

            def low_bits(s):
                folded(nc.vector.tensor_scalar(bits, bits, 0xFFF, None, ALU.bitwise_and))
                nc.vector.tensor_reduce(lowf[:, s:s + 1], bits, AX.X, ALU.max).then_inc(lowf_done, 1)

            def flag_out(s):
                dve.wait_ge(flagsum, s + 1)
                nc.vector.tensor_scalar(flag[:, s:s + 1], rows[0:1, 0, s:s + 1], 0.0, None, ALU.is_gt).then_inc(flag_done, 1)

            for f in range(NB):
                dve.wait_ge(kv_ready, f + 1)
                if f >= 2:
                    dve.wait_ge(et_ready, f - 1)
                nc.vector.tensor_copy(kv[f % 2], acc[:, f % 2, :]).then_inc(kv_out, 1)
            dve.wait_ge(et_ready, NB)
            nc.vector.tensor_copy(ET[:, :], acc[0:D, 2, 0:D]).then_inc(et_out, 1)
            dve.wait_ge(t1_ready, 1)
            nc.vector.tensor_scalar(T1[:, :], acc[0:D, 3, 0:E], CTX_SCALE, None, ALU.mult).then_inc(t1_out, 1)
            dve.wait_ge(m_ready, 1)
            nc.vector.tensor_copy(M[:, :, :], rows[:, 0:4:2, :]).then_inc(m_out, 1)

            def stats(ln, n, par):
                y = xbuf[:, 2 + par, :].rearrange("p (t e) -> p t e", e=E)
                dve.wait_ge(sum_done[ln], n)
                for q in range(TPB):
                    last = nc.vector.bn_stats(st[ln][:, q, :], y[:, q, :])
                last.then_inc(stats_done[ln], 1)
                dve.wait_ge(cst_in, 16 * NCST)
                dve.wait_ge(stats_done[ln], n)
                for q in range(TPB):
                    last = nc.vector.bn_aggr(mv[ln][:, q, :], st[ln][:, q, :])
                last.then_inc(aggr_done[ln], 1)

            def normalise(ln, n, par):
                y = xbuf[:, 2 + par, :].rearrange("p (t e) -> p t e", e=E)
                dve.wait_ge(rstd_done[ln], n)
                for q in range(TPB):
                    last = nc.vector.tensor_scalar(y[:, q, :], y[:, q, :], mv[ln][:, q, 0:1], rstd[ln][:, q:q + 1],
                                                   ALU.subtract, ALU.mult)
                last.then_inc(norm_done[ln], 1)

            def residual1(b, par, loads, banks):
                dve.wait_ge(op_ready, b + 1)
                dve.wait_ge(xf_in[2 + par], loads * 16)
                nc.vector.tensor_tensor(xbuf[:, 2 + par, :], banks,
                                        xbuf[:, 2 + par, :], ALU.add).then_inc(sum_done[0], 1)

            def residual2(b, par):
                dve.wait_ge(w3_ready, b + 1)
                nc.vector.tensor_tensor(scaled[:, :, :], rows[:, :, :],
                                        s3b[:, :].unsqueeze(1).broadcast_to([P, TPB, E]), ALU.mult).then_inc(w3_used, 1)
                dve.wait_ge(w3_used, b + 1)
                nc.vector.tensor_tensor(xbuf[:, 2 + par, :], scaled[:, :, :].rearrange("p t e -> p (t e)"),
                                        xbuf[:, 2 + par, :], ALU.add).then_inc(sum_done[1], 1)

            def lo_of_transposed(b):
                for c in range(EC):
                    dve.wait_ge(trhi_done, b * EC + (c + 1))
                    nc.vector.tensor_tensor(x1T[:, 1, c, :], trp[:, c, :], x1T[:, 0, c, :].bitcast(f32),
                                            ALU.subtract).then_inc(trlo_done, 1)

            def lo_part(b, n, dst, j):
                dve.wait_ge(hi_done, b * SPLITS + (n + 1))
                nc.vector.tensor_tensor(dst[:, 1, j, :], g[:, n % NG, :], dst[:, 0, j, :].bitcast(f32),
                                        ALU.subtract).then_inc(split_done, 1)

            row_banks = rows[:, :, :].rearrange("p t e -> p (t e)")
            spare_banks = acc[:, 2:4, :].rearrange("p a n -> p (a n)")

            def gated(b, par, first):
                for j in range(HC + 1):
                    if j < HC:
                        dve.wait_ge(silu_done, b * HC + (j + 1))
                        dve.wait_ge(tile_ready, b * TILES + (2 * j + 2))
                        if j >= NG or not first:
                            dve.wait_ge(split_done, b * SPLITS + (j - NG + 1))
                        nc.vector.scalar_tensor_tensor(g[:, j % NG, :], acc[:, (2 * j + 1) % RING, :], sc[:, 1, j:j + 1],
                                                       sg[:, j % 2, :], ALU.mult, ALU.mult).then_inc(h_made, 1)
                    if j >= 1:
                        if not first:
                            lo_part(b, j - 1, hid[par], j - 1)
                    if first and j < HC:
                        fold(CH_L1, CH_L1 + j)

            def turn(b, par, loads, more, first=False):
                nxt = 1 - par
                gated(b, par, first)
                if first:
                    low_bits(1)
                    flag_out(1)
                    stats(0, 2, 1)
                else:
                    residual2(b - 1, nxt)
                    stats(1, b, nxt)
                for j in range(HC):
                    lo_part(b, HC + j, hid[nxt], j)
                    if j == 0 and not first:
                        normalise(1, b, nxt)
                    if j == 0 and first:
                        normalise(0, 2, 1)
                    if first:
                        for k in ((0, 1), (2,), (3,), (4,), (5, 6), (7,), (), ())[j]:
                            fold(CH_H1, CH_H1 + k)
                        if j == FLAG2_AFTER - 1:
                            low_bits(2)
                        if j == FLAG2_AFTER:
                            flag_out(2)
                if more and not first:
                    residual1(b + 1, nxt, loads, row_banks)
                    stats(0, b + 2, nxt)
                for j in range(HC):
                    if j == HC - 1:
                        dve.wait_ge(hi_done, b * SPLITS + SPLITS)
                        nc.vector.tensor_copy(hid[par][:, 0, j, :], g[:, (SPLITS - 1) % NG, :]).then_inc(last_hi_done, 1)
                        dve.wait_ge(last_hi_done, b + 1)
                    lo_part(b, 2 * HC + j, hid[par], j)
                    if j == 0 and more and not first:
                        normalise(0, b + 2, nxt)
                    if first and j == 2:
                        fold(CH_H2, CH_H2 + 1)
                        low_bits(3)
                    if first and j == TR_AFTER:
                        flag_out(3)
                    if j == TR_AFTER + 1 and more:
                        lo_of_transposed(b + 1)

            for i in range(CH_L1):
                fold(0, i)
            residual1(0, 0, 2 + 1, row_banks)
            stats(0, 1, 0)
            low_bits(0)
            normalise(0, 1, 0)
            flag_out(0)
            residual1(1, 1, 2 + 1, spare_banks)
            lo_of_transposed(0)
            turn(0, 0, 0, True, first=True)
            with dve.Fori(0, (NB - 2) // 2) as i:
                turn(i * 2 + 1, 1, i + 4, True)
                turn(i * 2 + 2, 0, i + 4, True)
            turn(NB - 1, 1, 0, False)
            y = xbuf[:, 3, :].rearrange("p (t e) -> p t e", e=E)

            def tail_normalise(q):
                dve.wait_ge(tail_rstd_done, q + 1)
                nc.vector.tensor_scalar(y[:, q, :], y[:, q, :], mv[1][:, q, 0:1], rstd[1][:, q:q + 1],
                                        ALU.subtract, ALU.mult).then_inc(tail_done, 1)

            for q in range(TPB):
                dve.wait_ge(w3_ready, NB + q)
                nc.vector.tensor_tensor(scaled[:, q, :], acc[:, q, 0:E], s3b[:, :], ALU.mult).then_inc(tail_scaled, 1)
                dve.wait_ge(tail_scaled, q + 1)
                nc.vector.tensor_tensor(y[:, q, :], scaled[:, q, :], y[:, q, :], ALU.add).then_inc(tail_sum, 1)
                dve.wait_ge(tail_sum, q + 1)
                nc.vector.bn_stats(st[1][:, q, :], y[:, q, :]).then_inc(tail_stats, 1)
                dve.wait_ge(tail_stats, q + 1)
                nc.vector.bn_aggr(mv[1][:, q, :], st[1][:, q, :]).then_inc(tail_aggr, 1)
                if q >= 1:
                    tail_normalise(q - 1)
            tail_normalise(TPB - 1)

        @block.tensor
        def _(pe):
            def kv_products(f):
                pe.wait_ge(xf_in[f % 4], 16 * (f // 4 + 1))
                if f >= 2:
                    pe.wait_ge(kv_out, f - 1)
                xt = xbuf[:, f % 4, :].rearrange("p (c t n) -> p c t n", c=EC, t=TPB)
                for q in range(TPB):
                    for c in range(EC):
                        last = nc.tensor.matmul(acc[:, f % 2, q * P:(q + 1) * P], xt[:, c, q, :], wkv[:, c, :],
                                                start=c == 0, stop=c == EC - 1)
                last.then_inc(kv_ready, 1)

            def energy(f):
                pe.wait_ge(kv_out, f + 1)
                for q in range(TPB):
                    k, v = kv[f % 2][:, q * P:q * P + D], kv[f % 2][:, q * P + D:(q + 1) * P]
                    last = nc.tensor.matmul(acc[0:D, 2, 0:D], v, k, start=(f == 0 and q == 0),
                                            stop=(f == NB - 1 and q == TPB - 1))
                last.then_inc(et_ready, 1)

            pe.wait_ge(wkv_in, 16)
            kv_products(0)
            for f in range(NB):
                if f + 1 < NB:
                    kv_products(f + 1)
                energy(f)
            pe.wait_ge(cst_in, 16 * NCST)
            pe.wait_ge(et_out, 1)
            nc.tensor.matmul(acc[0:D, 3, 0:E], ET[:, :], wo[:, :], start=True, stop=True).then_inc(t1_ready, 1)
            pe.wait_ge(t1_out, 1)
            for c in range(EC):
                last = nc.tensor.matmul(rows[:, 2 * c, :], wq[:, c * P:(c + 1) * P], T1[:, :], start=True, stop=True)
            last.then_inc(m_ready, 1)
            pe.wait_ge(m_out, 1)

            spare = acc[:, 2:4, :].rearrange("p a (t e) -> p (a t) e", e=E)

            def attention_out(b, par, loads, to):
                pe.wait_ge(xf_in[par], loads * 16)
                xt = xbuf[:, par, :].rearrange("p (c t n) -> p c t n", c=EC, t=TPB)
                for q in range(TPB):
                    for c in range(EC):
                        last = nc.tensor.matmul(to[:, q, :], xt[:, c, q, :], M[:, c, :], start=c == 0, stop=c == EC - 1)
                last.then_inc(op_ready, 1)

            def transposes(b, par):
                pe.wait_ge(norm_done[0], b + 1)
                y = xbuf[:, 2 + par, :].rearrange("p (t e) -> p t e", e=E)
                for c in range(EC):
                    for q in range(TPB):
                        last = nc.tensor.transpose(trp[:, c, q * P:(q + 1) * P], y[:, q, c * P:(c + 1) * P], ident[:, :])
                last.then_inc(tr_ready, 1)

            def flag_sum(s):
                pe.wait_ge(lowf_done, s + 1)
                nc.tensor.matmul(rows[0:1, 0, s:s + 1], lowf[:, s:s + 1], ones[:, :], start=True, stop=True).then_inc(flagsum, 1)

            inexact = [None] * 4

            def load_flag(s):
                pe.wait_ge(flag_done, s + 1)
                inexact[s] = pe.value_load(flag[0:1, s:s + 1], min_val=0, max_val=1)

            def either(s, stage_of):
                with pe.If(inexact[s] == 0):
                    stage_of(lambda ap: ap)
                with pe.Else():
                    stage_of(lambda ap: ap.bitcast(f32))

            def tile_free(b, t, after_previous):
                u = t - RING
                if u < 0:
                    if after_previous:
                        pe.wait_ge(hi_done, (b - 1) * SPLITS + (u + TILES - HC + 1))
                elif u < 2 * HC:
                    pe.wait_ge(silu_done if u % 2 == 0 else h_made, b * HC + (u // 2 + 1))
                else:
                    pe.wait_ge(hi_done, b * SPLITS + (u - HC + 1))

            def stage_l1(b, par, view, after_previous):
                for t in range(2 * HC):
                    j, at = t // 2, (W1_AT, W2_AT)[t % 2]
                    tile_free(b, t, after_previous)
                    for c in range(EC):
                        w = view(W[:, at + c * HID + j * P:at + c * HID + (j + 1) * P])
                        for part in range(2):
                            last = nc.tensor.matmul(acc[:, t % RING, :], w, view(x1T[:, part, c, :]),
                                                    start=c == 0 and part == 0, stop=c == EC - 1 and part == 1)
                    last.then_inc(tile_ready, 1)

            def stage_hidden(b, layer, src, view, js, between=None):
                at = (H1_AT, H2_AT)[layer - 1]
                for j in js:
                    t = (layer + 1) * HC + j
                    tile_free(b, t, True)
                    for k in range(HC):
                        if j == 0:
                            pe.wait_ge(split_done, b * SPLITS + ((layer - 1) * HC + k + 1))
                        w = view(W[:, at + k * HID + j * P:at + k * HID + (j + 1) * P])
                        for part in range(2):
                            last = nc.tensor.matmul(acc[:, t % RING, :], w, view(src[:, part, k, :]),
                                                    start=k == 0 and part == 0, stop=k == HC - 1 and part == 1)
                    last.then_inc(tile_ready, 1)

            def stage_w3(b, src, view):
                for q0 in range(TPB // 2):
                    for k in range(HC):
                        if q0 == 0:
                            pe.wait_ge(split_done, b * SPLITS + (2 * HC + k + 1))
                        w = view(W[:, W3_AT + k * E:W3_AT + (k + 1) * E])
                        for q in (q0, q0 + 2):
                            for part in range(2):
                                last = nc.tensor.matmul(rows[:, q, :], view(src[:, part, k, q * P:(q + 1) * P]), w,
                                                        start=k == 0 and part == 0, stop=k == HC - 1 and part == 1)
                last.then_inc(w3_ready, 1)

            def last_w3(view):
                b, src = NB - 1, hid[1]
                for tiles in ((0, 1), (2,), (3,)):
                    for q in tiles:
                        pe.wait_ge(hi_done, b * SPLITS + (2 * HC + RING + q + 1))
                    for k in range(HC):
                        pe.wait_ge(split_done, b * SPLITS + (2 * HC + k + 1))
                        w = view(W[:, W3_AT + k * E:W3_AT + (k + 1) * E])
                        for q in tiles:
                            for part in range(2):
                                last = nc.tensor.matmul(acc[:, q, 0:E], view(src[:, part, k, q * P:(q + 1) * P]), w,
                                                        start=k == 0 and part == 0, stop=k == HC - 1 and part == 1)
                            if k == HC - 1:
                                last.then_inc(w3_ready, 1)

            def down(b, par):
                pe.wait_ge(sum_done[0], b + 2)
                either(3, lambda view: stage_w3(b, hid[par], view))

            def turn(b, par, loads, more, first=False):
                nxt = 1 - par
                pe.wait_ge(trlo_done, (b + 1) * EC)
                if first:
                    pe.wait_ge(sum_done[0], 2)
                either(0, lambda view: stage_l1(b, par, view, not first))
                if first:
                    flag_sum(1)
                    load_flag(1)
                    for i in range(CH_L1, CH_H1):
                        chunk_landed(pe, i)
                else:
                    down(b - 1, nxt)
                cut = FLAG2_AFTER + 1 if first else HC
                either(1, lambda view: stage_hidden(b, 1, hid[par], view, range(cut)))
                if first:
                    flag_sum(2)
                    either(1, lambda view: stage_hidden(b, 1, hid[par], view, range(cut, HC)))
                    load_flag(2)
                    for i in range(CH_H1, CH_H2):
                        chunk_landed(pe, i)
                elif more:
                    pe.wait_ge(w3_used, b)
                    attention_out(b + 1, nxt, loads, rows)
                cut = TR_AFTER + 1
                either(2, lambda view: stage_hidden(b, 2, hid[nxt], view, range(cut)))
                if first:
                    flag_sum(3)
                if more:
                    transposes(b + 1, nxt)
                either(2, lambda view: stage_hidden(b, 2, hid[nxt], view, range(cut, HC)))
                if first:
                    load_flag(3)
                    for i in range(CH_H2, CH_W3):
                        chunk_landed(pe, i)

            pe.wait_ge(made, 5)
            attention_out(0, 0, 2 + 1, rows)
            attention_out(1, 1, 2 + 1, spare)
            flag_sum(0)
            transposes(0, 0)
            load_flag(0)
            for i in range(CH_L1):
                chunk_landed(pe, i)
            turn(0, 0, 0, True, first=True)
            with pe.Fori(0, (NB - 2) // 2) as i:
                turn(i * 2 + 1, 1, i + 4, True)
                turn(i * 2 + 2, 0, i + 4, True)
            turn(NB - 1, 1, 0, False)
            either(3, last_w3)


def kernel(**inputs):
    import numpy as np
    import concourse.bacc as bacc
    from concourse.bass_utils import run_bass_kernel_spmd

    def get(name):
        return np.asarray(inputs["L0_" + name])

    x = get("attn_x").reshape(P, NB, TPB, E)
    arrays = {
        "xT": x.reshape(P, NB, TPB, EC, P).transpose(4, 1, 3, 2, 0).reshape(P, TOK * EC),
        "x_rows": x.reshape(P, NB * TPB * E),
        "wkv": np.concatenate([get("attn_wk"), get("attn_wv")], 0).T.reshape(EC, P, 2 * D).transpose(1, 0, 2),
        "wq": get("attn_wq"),
        "woT": get("attn_wo").T,
        "w1T": get("ffn_w1_w").T.reshape(EC, P, HID).transpose(1, 0, 2).reshape(P, EC * HID),
        "w2T": get("ffn_w2_w").T.reshape(EC, P, HID).transpose(1, 0, 2).reshape(P, EC * HID),
        "h1T": get("ffn_h1_w").T.reshape(HC, P, HID).transpose(1, 0, 2).reshape(P, HC * HID),
        "h2T": get("ffn_h2_w").T.reshape(HC, P, HID).transpose(1, 0, 2).reshape(P, HC * HID),
        "w3T": get("ffn_w3_w").T.reshape(HC, P, E).transpose(1, 0, 2).reshape(P, HC * E),
        "scales": np.stack([get("ffn_" + n).reshape(HC, P) for n in ("w1_s", "w2_s", "h1_s", "h2_s")]).transpose(2, 0, 1),
        "s3": get("ffn_w3_s"),
    }
    arrays = {n: np.ascontiguousarray(a) for n, a in arrays.items()}
    nc = bacc.Bacc("TRN2", target_bir_lowering=False, num_devices=1)
    args = [nc.dram_tensor("in_" + n, a.shape, mybir.dt.from_np(a.dtype), kind="ExternalInput").ap() for n, a in arrays.items()]
    out = nc.dram_tensor("out", (P, NB * TPB * E), mybir.dt.float32, kind="ExternalOutput").ap()
    build(nc, *args, out)
    r = run_bass_kernel_spmd(nc, [{"in_" + n: a for n, a in arrays.items()}], core_ids=[0])
    return r.results[0]["out"].reshape(1, TOK, E)
```

```python
import math

import concourse.bass as bass
from concourse import mybir
from contextlib import ExitStack

P = 128
TOK, E, D, HID = 4096, 256, 64, 1024
BLK = 512
NB = TOK // BLK
NCST = 4
TPB = BLK // P
EC = E // P
HC = HID // P
EPS = 1e-5
CTX_SCALE = math.sqrt(3.0 / D)

W1_AT, W2_AT = 0, EC * HID
H1_AT = 2 * EC * HID
H2_AT = H1_AT + HC * HID
W3_AT = H2_AT + HC * HID
W_COLS = W3_AT + HC * E
WCH = 1024
NCH = W_COLS // WCH
CH_L1, CH_H1, CH_H2 = 4, 12, 20
EARLY = CH_H1
SLOTS = 8
LATE = 4
FRONT = [*range(2, NB), 0, 1]

H2_CHUNKS = [(12, 13), (14, 15), (16, 17), (18, 19), (), (), (), ()]
W3_CHUNKS = [(20, 21), (), (), (), (), (), (), ()]

RING = 4
TILES = 4 * HC
NG = 3
SPLITS = 3 * HC
FLAG1_AFTER = 6
MASK1_AFTER, MAX1_AFTER = 3, 4
FLAG2_AFTER = 6
LOW2_AFTER = 4
Q_AFTER = 3
HI0_AFTER = 9
WARM_START, WARM_TR, WARM_L1 = 7, 3, 4
TR_AFTER = 5


def build(nc, xT_in, xr_in, wkv_src, wq_in, wo_in, w1_in, w2_in, h1_in, h2_in, w3_in, sc_in, s3_in, out):
    f32, f32r, i32 = mybir.dt.float32, mybir.dt.float32r, mybir.dt.int32
    ALU, ACT, AX = mybir.AluOpType, mybir.ActivationFunctionType, mybir.AxisListType

    ctx = ExitStack()
    with ctx:
        def sb(name, shape, dt=f32):
            return ctx.enter_context(nc.sbuf_tensor(name, shape, dt))

        def sem(name):
            return ctx.enter_context(nc.semaphore(name))

        W = sb("W", [P, W_COLS], f32r)
        with nc.sbuf_tensor("stage", [P, SLOTS, WCH], f32) as stage:
            pass
        hid = [None, sb("hid1", [P, 2, HC, BLK], f32r)]
        hid[0] = sb("hid0", [P, 2, HC, BLK], f32r)
        x1T = sb("x1T", [P, 2, EC, BLK], f32r)
        xbuf = sb("xbuf", [P, 4, TPB * E])
        with ExitStack() as front:
            def early(name, shape, dt=f32):
                return front.enter_context(nc.sbuf_tensor(name, shape, dt))

            wkv = early("wkv", [P, EC, 2 * D])
            wo = early("wo", [D, E])
            ET = early("ET", [D, 2, D])
            T1 = early("T1", [2 * D, E])
            zeros = early("zeros", [P, BLK], mybir.dt.bfloat16)
        g = sb("g", [P, NG, BLK])
        late = sb("late", [P, LATE // 2, WCH])
        sg = sb("sg", [P, 2, BLK])
        scaled = sb("scaled", [P, TPB, E])
        qs = [sb(f"qs{i}", [P, BLK], f32r) for i in range(2)]
        T1s = sb("T1s", [2 * D, 2, E], f32r)
        wq = sb("wq", [P, EC, 2 * D])
        s3b = sb("s3b", [P, E])
        sc = sb("sc", [P, 4, HC])
        ident = sb("ident", [P, P])
        ones = sb("ones", [P, 1])
        nhalf = sb("nhalf", [P, TPB])
        eps = sb("eps", [P, TPB])
        st = [sb(f"st{i}", [P, TPB, 6]) for i in range(2)]
        mv = [sb(f"mv{i}", [P, TPB, 2]) for i in range(2)]
        ve = [sb(f"ve{i}", [P, TPB]) for i in range(2)]
        rstd = [sb(f"rstd{i}", [P, TPB]) for i in range(2)]
        lowf = sb("lowf", [P, 4])
        flag = sb("flag", [1, 4], i32)
        acc = ctx.enter_context(nc.psum_tensor("acc", [P, RING, BLK], f32))
        rows = ctx.enter_context(nc.psum_tensor("rows", [P, TPB, E], f32))
        trp = ctx.enter_context(nc.psum_tensor("trp", [P, EC, BLK], f32))
        scratch = nc.dram_tensor("scratch", (P, W_COLS), f32, kind="Internal").ap()
        kv = [scaled[:, 0:2, :].rearrange("p a e -> p (a e)"), scaled[:, 2:4, :].rearrange("p a e -> p (a e)")]

        wkv_in = sem("wkv_in")
        cst_in = sem("cst_in")
        zeros_made = sem("zeros_made")
        made = sem("made")
        xf_in = [sem(f"xf_in{i}") for i in range(4)]
        x_first = sem("x_first")
        staged = [sem(f"staged{i}") for i in range(SLOTS)]
        staged_late = [sem(f"staged_late{i}") for i in range(LATE)]
        copied = sem("copied")
        relayed = [sem(f"relayed{i}") for i in range(4)]
        reloaded = [sem(f"reloaded{i}") for i in range(4)]
        kv_ready, kv_out = sem("kv_ready"), sem("kv_out")
        et_ready, et_out = sem("et_ready"), sem("et_out")
        t1_ready, t1_out = sem("t1_ready"), sem("t1_out")
        t1_split = sem("t1_split")
        q_ready = sem("q_ready")
        qhi_done, qlo_done = sem("qhi_done"), sem("qlo_done")
        fold_done, lowf_done = sem("fold_done"), sem("lowf_done")
        flagsum, flag_done = sem("flagsum"), sem("flag_done")
        tile_ready = sem("tile_ready")
        silu_done = sem("silu_done")
        h_made = sem("h_made")
        hi_done = sem("hi_done")
        split_done = sem("split_done")
        op_ready, w3_ready, tr_ready = sem("op_ready"), sem("w3_ready"), sem("tr_ready")
        w3_used = sem("w3_used")
        trhi_done, trlo_done = sem("trhi_done"), sem("trlo_done")
        sum_done = [sem(f"sum_done{i}") for i in range(2)]
        stats_done = [sem(f"stats_done{i}") for i in range(2)]
        aggr_done = [sem(f"aggr_done{i}") for i in range(2)]
        ve_done = [sem(f"ve_done{i}") for i in range(2)]
        rstd_done = [sem(f"rstd_done{i}") for i in range(2)]
        norm_done = [sem(f"norm_done{i}") for i in range(2)]
        stored = sem("stored")
        op_tile = sem("op_tile")
        last_hi_done = sem("last_hi_done")
        tile_scaled = sem("tile_scaled")
        tile_sum = [sem(f"tile_sum{i}") for i in range(2)]
        tile_stats = [sem(f"tile_stats{i}") for i in range(2)]
        tile_aggr = [sem(f"tile_aggr{i}") for i in range(2)]
        tile_ve = [sem(f"tile_ve{i}") for i in range(2)]
        tile_rstd = [sem(f"tile_rstd{i}") for i in range(2)]
        tile_norm = [sem(f"tile_norm{i}") for i in range(2)]

        weight_of = ([(w1_in, c) for c in range(EC)] + [(w2_in, c) for c in range(EC)]
                     + [(h1_in, k) for k in range(HC)] + [(h2_in, k) for k in range(HC)]
                     + [(w3_in, c) for c in range(HC * E // WCH)])

        FIRST = (0, CH_L1, CH_H1, CH_H2, NCH)

        def slot_of(i):
            if i < EARLY:
                k = i % SLOTS
                return stage[:, k, :], staged[k], 16 * (i // SLOTS + 1), i - SLOTS if i >= SLOTS else None
            n = i - EARLY
            k = n % LATE
            slot = late[:, k, :] if k < LATE // 2 else xbuf[:, 2 + k - LATE // 2, :]
            return slot, staged_late[k], 16 * (n // LATE + 1), i - LATE if n >= LATE else None

        def folds_until(i):
            first = max(f for f in FIRST if f <= i)
            return first + max(i - first, 1)

        def chunk_used(eng, i):
            eng.wait_ge(copied, i + 1)
            eng.wait_ge(fold_done, folds_until(i))

        def flag_at(s):
            if s == 0:
                return acc[0:1, 0, 0:1]
            return trp[0:1, 0, 0:1] if s == 1 else rows[0:1, 0, s:s + 1]

        block = ctx.enter_context(nc.Block())

        @block.sync
        def _(sp):
            sp.dma_start(wkv[:, :, :], wkv_src).then_inc(wkv_in, 16)

            def load(i):
                slot, arrived, _, before = slot_of(i)
                if before is not None:
                    chunk_used(sp, before)
                src, c = weight_of[i]
                sp.dma_start(slot, src[:, c * WCH:(c + 1) * WCH]).then_inc(arrived, 16)

            def load_x(f, slot, src):
                sp.dma_start(xbuf[:, slot, :], src[:, f * TPB * E:(f + 1) * TPB * E]).then_inc(xf_in[slot], 16)

            at = FRONT[0] * TPB * E
            sp.dma_start(xbuf[:, 0, 0:E], xT_in[:, at:at + E]).then_inc(x_first, 16)
            sp.dma_start(xbuf[:, 0, E:TPB * E], xT_in[:, at + E:at + TPB * E]).then_inc(xf_in[0], 16)
            for n in range(1, 4):
                load_x(FRONT[n], n, xT_in)
            for dst, src in ((wo[:, :], wo_in), (wq[:, :, :], wq_in), (sc[:, :, :], sc_in), (s3b[:, :], s3_in.partition_broadcast(P))):
                sp.dma_start(dst, src).then_inc(cst_in, 16)
            for n in range(4, NB):
                if n < 6:
                    load(n - 4)
                sp.wait_ge(kv_ready, n - 3)
                load_x(FRONT[n], n % 4, xT_in)
            for i in range(2, CH_L1):
                load(i)
            for b in range(2):
                sp.wait_ge(kv_ready, 5 + b)
                load_x(b, b, xr_in)
            for i in range(CH_L1, CH_L1 + 4):
                load(i)

            def reload(s):
                sp.wait_ge(flag_done, s + 1)
                whole = sp.value_load(flag[0:1, s:s + 1], min_val=0, max_val=1)
                with sp.If(whole == 1):
                    for i in range(FIRST[s], FIRST[s + 1]):
                        src, c = weight_of[i]
                        sp.dma_start(scratch[:, i * WCH:(i + 1) * WCH], src[:, c * WCH:(c + 1) * WCH]).then_inc(relayed[s], 16)
                    sp.wait_ge(relayed[s], 16 * (FIRST[s + 1] - FIRST[s]))
                    sp.dma_start(W[:, FIRST[s] * WCH:FIRST[s + 1] * WCH].bitcast(f32),
                                 scratch[:, FIRST[s] * WCH:FIRST[s + 1] * WCH]).then_inc(reloaded[s], 16)

            for i in range(CH_L1 + 4, EARLY + LATE):
                if i == EARLY + LATE // 2:
                    sp.wait_ge(q_ready, 2)
                load(i)
            reload(0)
            reload(1)
            for i in range(EARLY + LATE, NCH):
                load(i)
            reload(2)
            reload(3)
            chunk_used(sp, NCH - 1)

            def turn(b, par, more):
                nxt = 1 - par
                if more:
                    sp.wait_ge(q_ready, b)
                    sp.dma_start(xbuf[:, 2 + nxt, :], xT_in[:, bass.ds((b + 1) * TPB * E, TPB * E)]).then_inc(xf_in[2 + nxt], 16)
                sp.wait_ge(norm_done[1], b)
                sp.dma_start(out[:, bass.ds((b - 1) * TPB * E, TPB * E)], xbuf[:, nxt, :]).then_inc(stored, 16)
                if more:
                    sp.wait_ge(stored, b * 16)
                    sp.dma_start(xbuf[:, nxt, :], xr_in[:, bass.ds((b + 1) * TPB * E, TPB * E)]).then_inc(xf_in[nxt], 16)

            with sp.Fori(0, (NB - 2) // 2) as i:
                turn(i * 2 + 1, 1, True)
                turn(i * 2 + 2, 0, True)
            turn(NB - 1, 1, False)
            for q in range(TPB):
                sp.wait_ge(tile_norm[1], q + 1)
                at = (NB - 1) * TPB * E + q * E
                sp.dma_start(out[:, at:at + E], xbuf[:, 1, q * E:(q + 1) * E]).then_inc(stored, 16)
            sp.wait_ge(stored, (NB - 1 + TPB) * 16)

        @block.gpsimd
        def _(pool):
            nc.gpsimd.memset(ident[:, :], 0.0).then_inc(made, 1)
            pool.wait_ge(made, 1)
            nc.gpsimd.affine_select(out=ident[:, :], in_=ident[:, :], compare_op=ALU.not_equal, fill=1.0, base=0,
                                    pattern=[[-1, P]], channel_multiplier=1).then_inc(made, 1)
            nc.gpsimd.memset(ones[:, :], 1.0).then_inc(made, 1)
            nc.gpsimd.memset(nhalf[:, :], -0.5).then_inc(made, 1)
            nc.gpsimd.memset(eps[:, :], EPS).then_inc(made, 1)
            pool.wait_ge(made, 5)

            def inverse_deviation(ln, n):
                pool.wait_ge(aggr_done[ln], n)
                nc.gpsimd.tensor_tensor(ve[ln][:, :], mv[ln][:, :, 1], eps[:, :], ALU.add).then_inc(ve_done[ln], 1)
                pool.wait_ge(ve_done[ln], n)
                nc.gpsimd.tensor_tensor(rstd[ln][:, :], ve[ln][:, :], nhalf[:, :], ALU.pow).then_inc(rstd_done[ln], 1)

            def inverse_deviation_tilewise(ln):
                for q in range(TPB):
                    pool.wait_ge(tile_aggr[ln], q + 1)
                    nc.gpsimd.tensor_tensor(ve[ln][:, q:q + 1], mv[ln][:, q, 1:2], eps[:, 0:1], ALU.add).then_inc(tile_ve[ln], 1)
                    pool.wait_ge(tile_ve[ln], q + 1)
                    nc.gpsimd.tensor_tensor(rstd[ln][:, q:q + 1], ve[ln][:, q:q + 1], nhalf[:, 0:1], ALU.pow).then_inc(tile_rstd[ln], 1)

            inverse_deviation_tilewise(0)
            for j in range(HC):
                pool.wait_ge(hi_done, j + 1)
                nc.gpsimd.tensor_tensor(hid[0][:, 1, j, :], g[:, j % NG, :], hid[0][:, 0, j, :].bitcast(f32),
                                        ALU.subtract).then_inc(split_done, 1)
            inverse_deviation(0, 1)
            with pool.Fori(0, NB - 2) as i:
                inverse_deviation(1, i + 1)
                inverse_deviation(0, i + 2)
            inverse_deviation(1, NB - 1)
            inverse_deviation_tilewise(1)

        @block.scalar
        def _(act):
            def copy_chunk(i):
                slot, arrived, value, _ = slot_of(i)
                act.wait_ge(arrived, value)
                nc.scalar.copy(W[:, i * WCH:(i + 1) * WCH], slot).then_inc(copied, 1)

            def hi_of_transposed(b):
                act.wait_ge(tr_ready, b + 1)
                for c in range(EC):
                    nc.scalar.copy(x1T[:, 0, c, :], trp[:, c, :]).then_inc(trhi_done, 1)

            def hi_of_q(b, par, bank=0):
                act.wait_ge(q_ready, b + 1)
                nc.scalar.copy(qs[par][:, :], trp[:, bank, :]).then_inc(qhi_done, 1)

            def gated(b, par):
                dst = hid[par]
                for j in range(HC + 1):
                    if j < HC:
                        act.wait_ge(tile_ready, b * TILES + (2 * j + 1))
                        if j >= 2:
                            act.wait_ge(h_made, b * HC + (j - 1))
                        nc.scalar.activation(sg[:, j % 2, :], acc[:, (2 * j) % RING, :], ACT.Silu,
                                             scale=sc[:, 0, j:j + 1]).then_inc(silu_done, 1)
                    if j >= 1:
                        act.wait_ge(h_made, b * HC + j)
                        nc.scalar.copy(dst[:, 0, j - 1, :], g[:, (j - 1) % NG, :]).then_inc(hi_done, 1)

            def hidden(b, layer, dst, transposed_next=None, chunks=None):
                for j in range(HC):
                    n = layer * HC + j
                    t = (layer + 1) * HC + j
                    act.wait_ge(tile_ready, b * TILES + (t + 1))
                    act.wait_ge(split_done, b * SPLITS + (n - NG + 1))
                    src = acc[:, t % RING, :]
                    whole = nc.scalar.activation(g[:, n % NG, :], src, ACT.Gelu, scale=sc[:, 1 + layer, j:j + 1])
                    if n == SPLITS - 1:
                        whole.then_inc(hi_done, 1)
                    else:
                        nc.scalar.activation(dst[:, 0, j, :], src, ACT.Gelu, scale=sc[:, 1 + layer, j:j + 1]).then_inc(hi_done, 1)
                    if transposed_next is not None and j == TR_AFTER:
                        hi_of_transposed(transposed_next)
                    if chunks:
                        for i in chunks[j]:
                            copy_chunk(i)

            def turn(b, par, more, first=False):
                gated(b, par)
                if more and not first:
                    hi_of_q(b + 1, 1 - par)
                hidden(b, 1, hid[1 - par], None, H2_CHUNKS if first else None)
                hidden(b, 2, hid[par], b + 1 if more else None, W3_CHUNKS if first else None)

            act.wait_ge(made, 5)
            nc.scalar.activation(rstd[1][:, 0:1], ones[:, :], ACT.Silu)
            for i in range(Q_AFTER):
                copy_chunk(i)
            hi_of_q(0, 0)
            hi_of_q(1, 1, 1)
            for i in range(Q_AFTER, HI0_AFTER):
                copy_chunk(i)
            act.wait_ge(cst_in, 16 * NCST)
            hi_of_transposed(0)
            for i in range(HI0_AFTER, CH_H1):
                copy_chunk(i)
            turn(0, 0, True, first=True)
            with act.Fori(0, (NB - 2) // 2) as i:
                turn(i * 2 + 1, 1, True)
                turn(i * 2 + 2, 0, True)
            turn(NB - 1, 1, False)

        @block.vector
        def _(dve):
            spare = sg[:, :, :].rearrange("p a n -> p (a n)").bitcast(i32)
            bits_of = [spare] + [scaled[:, :, :].rearrange("p t e -> p (t e)").bitcast(i32)] * 3
            folds = [0]

            def folded(instruction):
                folds[0] += 1
                instruction.then_inc(fold_done, 1)
                dve.wait_ge(fold_done, folds[0])

            def fold(s, i):
                if i > FIRST[s]:
                    w = []
                    for k in (i - 1, i) if i == FIRST[s] + 1 else (i,):
                        slot, arrived, value, _ = slot_of(k)
                        dve.wait_ge(arrived, value)
                        w.append(slot.bitcast(i32))
                    folded(nc.vector.tensor_tensor(bits_of[s], w[0] if len(w) > 1 else bits_of[s], w[-1], ALU.bitwise_or))

            def low_bits(s):
                mask(s)
                largest(s)

            def mask(s):
                folded(nc.vector.tensor_scalar(bits_of[s], bits_of[s], 0xFFF, None, ALU.bitwise_and))

            def largest(s):
                nc.vector.tensor_reduce(lowf[:, s:s + 1], bits_of[s], AX.X, ALU.max).then_inc(lowf_done, 1)

            def flag_out(s):
                dve.wait_ge(flagsum, s + 1)
                nc.vector.tensor_scalar(flag[:, s:s + 1], flag_at(s), 0.0, None, ALU.is_gt).then_inc(flag_done, 1)

            nc.vector.memset(zeros[:, :], 0.0).then_inc(zeros_made, 1)
            for f in range(NB):
                dve.wait_ge(kv_ready, f + 1)
                if f >= 2:
                    dve.wait_ge(et_ready, f - 1)
                nc.vector.tensor_copy(kv[f % 2], acc[:, f % 2, :]).then_inc(kv_out, 1)
                if 5 <= f < NB - 1:
                    fold(0, f - 4)
            dve.wait_ge(et_ready, NB)
            nc.vector.tensor_copy(ET[:, :, :], acc[0:D, 2, 0:D].unsqueeze(1).broadcast_to([D, 2, D])).then_inc(et_out, 1)
            fold(0, CH_L1 - 1)
            dve.wait_ge(t1_ready, 1)
            nc.vector.tensor_scalar(T1[:, :], acc[:, 3, 0:E], CTX_SCALE, None, ALU.mult).then_inc(t1_out, 1)
            dve.wait_ge(t1_out, 1)
            nc.vector.tensor_copy(T1s[:, 0, :], T1[:, :]).then_inc(t1_split, 1)
            dve.wait_ge(t1_split, 1)
            nc.vector.tensor_tensor(T1s[:, 1, :], T1[:, :], T1s[:, 0, :].bitcast(f32), ALU.subtract).then_inc(t1_split, 1)

            def lo_of_q(b, par, bank=0):
                lower = slice(D, 2 * D)
                dve.wait_ge(qhi_done, b + 1)
                nc.vector.tensor_tensor(qs[par][lower, :], trp[lower, bank, :], qs[par][lower, :].bitcast(f32),
                                        ALU.subtract).then_inc(qlo_done, 1)

            lo_of_q(0, 0)
            mask(0)

            def stats(ln, n, par):
                y = xbuf[:, par, :].rearrange("p (t e) -> p t e", e=E)
                dve.wait_ge(sum_done[ln], n)
                for q in range(TPB):
                    last = nc.vector.bn_stats(st[ln][:, q, :], y[:, q, :])
                last.then_inc(stats_done[ln], 1)
                dve.wait_ge(cst_in, 16 * NCST)
                dve.wait_ge(stats_done[ln], n)
                for q in range(TPB):
                    last = nc.vector.bn_aggr(mv[ln][:, q, :], st[ln][:, q, :])
                last.then_inc(aggr_done[ln], 1)

            def normalise(ln, n, par):
                y = xbuf[:, par, :].rearrange("p (t e) -> p t e", e=E)
                dve.wait_ge(rstd_done[ln], n)
                for q in range(TPB):
                    last = nc.vector.tensor_scalar(y[:, q, :], y[:, q, :], mv[ln][:, q, 0:1], rstd[ln][:, q:q + 1],
                                                   ALU.subtract, ALU.mult)
                last.then_inc(norm_done[ln], 1)

            def residual1(b, par, loads, banks):
                dve.wait_ge(op_ready, b + 1)
                dve.wait_ge(xf_in[par], loads * 16)
                nc.vector.tensor_tensor(xbuf[:, par, :], banks,
                                        xbuf[:, par, :], ALU.add).then_inc(sum_done[0], 1)

            def residual2(b, par):
                dve.wait_ge(w3_ready, b + 1)
                nc.vector.tensor_tensor(scaled[:, :, :], rows[:, :, :],
                                        s3b[:, :].unsqueeze(1).broadcast_to([P, TPB, E]), ALU.mult).then_inc(w3_used, 1)
                dve.wait_ge(w3_used, b + 1)
                nc.vector.tensor_tensor(xbuf[:, par, :], scaled[:, :, :].rearrange("p t e -> p (t e)"),
                                        xbuf[:, par, :], ALU.add).then_inc(sum_done[1], 1)

            def lo_of_transposed(b):
                for c in range(EC):
                    dve.wait_ge(trhi_done, b * EC + (c + 1))
                    nc.vector.tensor_tensor(x1T[:, 1, c, :], trp[:, c, :], x1T[:, 0, c, :].bitcast(f32),
                                            ALU.subtract).then_inc(trlo_done, 1)

            def lo_part(b, n, dst, j):
                dve.wait_ge(hi_done, b * SPLITS + (n + 1))
                nc.vector.tensor_tensor(dst[:, 1, j, :], g[:, n % NG, :], dst[:, 0, j, :].bitcast(f32),
                                        ALU.subtract).then_inc(split_done, 1)

            row_banks = rows[:, :, :].rearrange("p t e -> p (t e)")

            def gated(b, par, first):
                for j in range(HC + 1):
                    if j < HC:
                        dve.wait_ge(silu_done, b * HC + (j + 1))
                        dve.wait_ge(tile_ready, b * TILES + (2 * j + 2))
                        if j >= NG or not first:
                            dve.wait_ge(split_done, b * SPLITS + (j - NG + 1))
                        nc.vector.scalar_tensor_tensor(g[:, j % NG, :], acc[:, (2 * j + 1) % RING, :], sc[:, 1, j:j + 1],
                                                       sg[:, j % 2, :], ALU.mult, ALU.mult).then_inc(h_made, 1)
                    if j >= 1:
                        if not first:
                            lo_part(b, j - 1, hid[par], j - 1)
                    if first:
                        if j + 5 < HC:
                            fold(1, CH_L1 + j + 5)
                        if j == MASK1_AFTER:
                            mask(1)
                        if j == MAX1_AFTER:
                            largest(1)
                        if j == FLAG1_AFTER:
                            flag_out(1)

            def turn(b, par, loads, more, first=False):
                nxt = 1 - par
                gated(b, par, first)
                if first:
                    residual1(1, 1, 2 + 1, row_banks)
                    stats(0, 1, 1)
                else:
                    residual2(b - 1, nxt)
                    stats(1, b, nxt)
                for j in range(HC):
                    lo_part(b, HC + j, hid[nxt], j)
                    if j == 0 and not first:
                        normalise(1, b, nxt)
                        if more:
                            lo_of_q(b + 1, nxt)
                    if j == 0 and first:
                        normalise(0, 1, 1)
                    if first:
                        for i in H2_CHUNKS[j]:
                            fold(2, i)
                        if j == LOW2_AFTER:
                            low_bits(2)
                        if j == FLAG2_AFTER:
                            flag_out(2)
                if more and not first:
                    residual1(b + 1, nxt, loads, row_banks)
                    stats(0, b + 1, nxt)
                for j in range(HC):
                    if j == HC - 1:
                        dve.wait_ge(hi_done, b * SPLITS + SPLITS)
                        nc.vector.tensor_copy(hid[par][:, 0, j, :], g[:, (SPLITS - 1) % NG, :]).then_inc(last_hi_done, 1)
                        dve.wait_ge(last_hi_done, b + 1)
                    lo_part(b, 2 * HC + j, hid[par], j)
                    if j == 0 and more and not first:
                        normalise(0, b + 1, nxt)
                    if first:
                        for i in W3_CHUNKS[j]:
                            fold(3, i)
                        if j == 2:
                            low_bits(3)
                    if first and j == TR_AFTER:
                        flag_out(3)
                    if j == TR_AFTER and more:
                        lo_of_transposed(b + 1)

            def normalised_tilewise(ln, par, add, early):
                y = xbuf[:, par, :].rearrange("p (t e) -> p t e", e=E)

                def normalise_tile(q):
                    dve.wait_ge(tile_rstd[ln], q + 1)
                    nc.vector.tensor_scalar(y[:, q, :], y[:, q, :], mv[ln][:, q, 0:1], rstd[ln][:, q:q + 1],
                                            ALU.subtract, ALU.mult).then_inc(tile_norm[ln], 1)

                for q in range(TPB):
                    add(q, y[:, q, :]).then_inc(tile_sum[ln], 1)
                    dve.wait_ge(tile_sum[ln], q + 1)
                    nc.vector.bn_stats(st[ln][:, q, :], y[:, q, :]).then_inc(tile_stats[ln], 1)
                    dve.wait_ge(tile_stats[ln], q + 1)
                    nc.vector.bn_aggr(mv[ln][:, q, :], st[ln][:, q, :]).then_inc(tile_aggr[ln], 1)
                    if 1 <= q <= early:
                        normalise_tile(q - 1)
                    elif ln == 0:
                        lo_of_q(1, 1, 1)
                if ln == 0:
                    largest(0)
                for q in range(early, TPB):
                    normalise_tile(q)

            def attention_residual(q, y):
                dve.wait_ge(*((op_tile, q + 1) if q < TPB - 1 else (op_ready, 1)))
                return nc.vector.tensor_tensor(y, acc[:, q, 0:E], y, ALU.add)

            def down_residual(q, y):
                dve.wait_ge(w3_ready, NB + q)
                nc.vector.tensor_tensor(scaled[:, q, :], acc[:, q, 0:E], s3b[:, :], ALU.mult).then_inc(tile_scaled, 1)
                dve.wait_ge(tile_scaled, q + 1)
                return nc.vector.tensor_tensor(y, scaled[:, q, :], y, ALU.add)

            dve.wait_ge(xf_in[0], 16 * 3)
            normalised_tilewise(0, 0, attention_residual, TPB - 1)
            fold(1, CH_L1 + 1)
            flag_out(0)
            lo_of_transposed(0)
            for i in range(2, 5):
                fold(1, CH_L1 + i)
            turn(0, 0, 0, True, first=True)
            with dve.Fori(0, (NB - 2) // 2) as i:
                turn(i * 2 + 1, 1, i + 4, True)
                turn(i * 2 + 2, 0, i + 4, True)
            turn(NB - 1, 1, 0, False)
            normalised_tilewise(1, 1, down_residual, 1)

        @block.tensor
        def _(pe):
            def q_products(par, chunks, bank=0):
                xt = xbuf[:, 2 + par, :].rearrange("p (t c n) -> p t c n", c=EC, t=TPB)
                for c in chunks:
                    last = nc.tensor.matmul(trp[:, bank, :], wq[:, c, :], xt[:, :, c, :], start=c == 0, stop=c == EC - 1)
                    if c == EC - 1:
                        last.then_inc(q_ready, 1)

            def kv_products(f):
                if f == 0:
                    pe.wait_ge(x_first, 16)
                else:
                    pe.wait_ge(xf_in[f % 4], 16 * (f // 4 + 1))
                if f >= 2:
                    pe.wait_ge(kv_out, f - 1)
                xt = xbuf[:, f % 4, :].rearrange("p (t c n) -> p t c n", c=EC, t=TPB)
                for q in range(TPB):
                    if f == 0 and q == 1:
                        pe.wait_ge(xf_in[0], 16)
                    for c in range(EC):
                        last = nc.tensor.matmul(acc[:, f % 2, q * P:(q + 1) * P], xt[:, q, c, :], wkv[:, c, :],
                                                start=c == 0, stop=c == EC - 1)
                last.then_inc(kv_ready, 1)

            def energy(f):
                pe.wait_ge(kv_out, f + 1)
                for q in range(TPB):
                    k, v = kv[f % 2][:, q * P:q * P + D], kv[f % 2][:, q * P + D:(q + 1) * P]
                    last = nc.tensor.matmul(acc[0:D, 2, 0:D], v, k, start=(f == 0 and q == 0),
                                            stop=(f == NB - 1 and q == TPB - 1))
                last.then_inc(et_ready, 1)

            def keep_clock(n, bank):
                for _ in range(n):
                    nc.tensor.matmul(acc[:, bank, :], zeros[:, 0:P], zeros[:, :], start=True, stop=True)

            pe.wait_ge(zeros_made, 1)
            keep_clock(WARM_START, 3)
            pe.wait_ge(wkv_in, 16)
            kv_products(0)
            for f in range(NB - 1):
                kv_products(f + 1)
                energy(f)
            pe.wait_ge(cst_in, 16 * NCST)
            q_products(0, (0,))
            energy(NB - 1)
            q_products(0, (1,))
            pe.wait_ge(et_out, 1)
            nc.tensor.matmul(acc[:, 3, 0:E], ET[:, :, :].rearrange("p a d -> p (a d)"), wo[:, :],
                             start=True, stop=True).then_inc(t1_ready, 1)
            q_products(1, (0, 1), 1)

            def attention_out(b, par, to, tilewise=False):
                pe.wait_ge(qlo_done, b + 1)
                for q in range(TPB):
                    for part in range(2):
                        if tilewise and q == 0:
                            pe.wait_ge(t1_split, part + 1)
                        last = nc.tensor.matmul(to[:, q, :], qs[par][:, q * P:(q + 1) * P], T1s[:, part, :],
                                                start=part == 0, stop=part == 1)
                    if tilewise and q < TPB - 1:
                        last.then_inc(op_tile, 1)
                last.then_inc(op_ready, 1)

            def transposes(b, par, tilewise=False):
                if not tilewise:
                    pe.wait_ge(norm_done[0], b)
                y = xbuf[:, par, :].rearrange("p (t e) -> p t e", e=E)
                for q in range(TPB):
                    if tilewise:
                        pe.wait_ge(tile_norm[0], q + 1)
                    for c in range(EC):
                        last = nc.tensor.transpose(trp[:, c, q * P:(q + 1) * P], y[:, q, c * P:(c + 1) * P], ident[:, :])
                    if tilewise and q < TPB - 1:
                        keep_clock(WARM_TR, 0)
                last.then_inc(tr_ready, 1)

            def flag_sum(s):
                pe.wait_ge(lowf_done, s + 1)
                nc.tensor.matmul(flag_at(s), lowf[:, s:s + 1], ones[:, :], start=True, stop=True).then_inc(flagsum, 1)

            inexact = [None] * 4

            def load_flag(s):
                pe.wait_ge(flag_done, s + 1)
                inexact[s] = pe.value_load(flag[0:1, s:s + 1], min_val=0, max_val=1)

            def either(s, stage_of):
                with pe.If(inexact[s] == 0):
                    stage_of(lambda ap: ap)
                with pe.Else():
                    pe.wait_ge(reloaded[s], 16)
                    stage_of(lambda ap: ap.bitcast(f32))

            def tile_free(b, t, after_previous):
                u = t - RING
                if u < 0:
                    if after_previous:
                        pe.wait_ge(hi_done, (b - 1) * SPLITS + (u + TILES - HC + 1))
                elif u < 2 * HC:
                    pe.wait_ge(silu_done if u % 2 == 0 else h_made, b * HC + (u // 2 + 1))
                else:
                    pe.wait_ge(hi_done, b * SPLITS + (u - HC + 1))

            def stage_l1(b, par, view, after_previous, ts):
                for t in ts:
                    j, at = t // 2, (W1_AT, W2_AT)[t % 2]
                    tile_free(b, t, after_previous)
                    for c in range(EC):
                        if t == 0:
                            pe.wait_ge(trlo_done, b * EC + (c + 1))
                        w = view(W[:, at + c * HID + j * P:at + c * HID + (j + 1) * P])
                        for part in range(2):
                            last = nc.tensor.matmul(acc[:, t % RING, :], w, view(x1T[:, part, c, :]),
                                                    start=c == 0 and part == 0, stop=c == EC - 1 and part == 1)
                    last.then_inc(tile_ready, 1)

            def stage_hidden(b, layer, src, view, js):
                at = (H1_AT, H2_AT)[layer - 1]
                for j in js:
                    t = (layer + 1) * HC + j
                    tile_free(b, t, True)
                    for k in range(HC):
                        if j == 0:
                            pe.wait_ge(split_done, b * SPLITS + ((layer - 1) * HC + k + 1))
                        w = view(W[:, at + k * HID + j * P:at + k * HID + (j + 1) * P])
                        for part in range(2):
                            last = nc.tensor.matmul(acc[:, t % RING, :], w, view(src[:, part, k, :]),
                                                    start=k == 0 and part == 0, stop=k == HC - 1 and part == 1)
                    last.then_inc(tile_ready, 1)

            def stage_w3(b, src, view):
                for q0 in range(TPB // 2):
                    for k in range(HC):
                        if q0 == 0:
                            pe.wait_ge(split_done, b * SPLITS + (2 * HC + k + 1))
                        w = view(W[:, W3_AT + k * E:W3_AT + (k + 1) * E])
                        for q in (q0, q0 + 2):
                            for part in range(2):
                                last = nc.tensor.matmul(rows[:, q, :], view(src[:, part, k, q * P:(q + 1) * P]), w,
                                                        start=k == 0 and part == 0, stop=k == HC - 1 and part == 1)
                last.then_inc(w3_ready, 1)

            def last_w3(view):
                b, src = NB - 1, hid[1]
                half = HC // 2
                for q, ks in ((0, range(HC - 1)), (1, range(half)), (0, range(HC - 1, HC)), (1, range(half, HC)),
                              (2, range(HC)), (3, range(HC))):
                    pe.wait_ge(hi_done, b * SPLITS + (2 * HC + RING + q + 1))
                    for k in ks:
                        if q < 2:
                            pe.wait_ge(split_done, b * SPLITS + (2 * HC + k + 1))
                        w = view(W[:, W3_AT + k * E:W3_AT + (k + 1) * E])
                        for part in range(2):
                            last = nc.tensor.matmul(acc[:, q, 0:E], view(src[:, part, k, q * P:(q + 1) * P]), w,
                                                    start=k == 0 and part == 0, stop=k == HC - 1 and part == 1)
                    if ks[-1] == HC - 1:
                        last.then_inc(w3_ready, 1)

            def down(b, par):
                pe.wait_ge(sum_done[0], b + 1)
                either(3, lambda view: stage_w3(b, hid[par], view))

            def turn(b, par, loads, more, first=False):
                nxt = 1 - par
                cut = 2 * (FLAG1_AFTER + 1) if first else 2 * HC
                either(0, lambda view: stage_l1(b, par, view, not first, range(cut)))
                if first:
                    flag_sum(1)
                    either(0, lambda view: stage_l1(b, par, view, False, range(cut, 2 * HC)))
                    load_flag(1)
                    pe.wait_ge(copied, CH_H1)
                else:
                    down(b - 1, nxt)
                    if more:
                        pe.wait_ge(xf_in[2 + nxt], loads * 16)
                        q_products(nxt, range(EC))
                cut = FLAG2_AFTER + 1 if first else HC
                either(1, lambda view: stage_hidden(b, 1, hid[par], view, range(cut)))
                if first:
                    pe.wait_ge(sum_done[0], 1)
                    flag_sum(2)
                    either(1, lambda view: stage_hidden(b, 1, hid[par], view, range(cut, HC)))
                    load_flag(2)
                    pe.wait_ge(copied, CH_H2)
                elif more:
                    pe.wait_ge(w3_used, b)
                    attention_out(b + 1, nxt, rows)
                cut = TR_AFTER + 1
                either(2, lambda view: stage_hidden(b, 2, hid[nxt], view, range(cut)))
                if first:
                    flag_sum(3)
                if more:
                    transposes(b + 1, nxt)
                either(2, lambda view: stage_hidden(b, 2, hid[nxt], view, range(cut, HC)))
                if first:
                    load_flag(3)
                    pe.wait_ge(copied, NCH)

            pe.wait_ge(made, 5)
            attention_out(0, 0, acc[:, :, 0:E], tilewise=True)
            attention_out(1, 1, rows)
            transposes(0, 0, tilewise=True)
            flag_sum(0)
            keep_clock(WARM_L1, 1)
            load_flag(0)
            pe.wait_ge(copied, CH_L1)
            turn(0, 0, 0, True, first=True)
            with pe.Fori(0, (NB - 2) // 2) as i:
                turn(i * 2 + 1, 1, i + 3, True)
                turn(i * 2 + 2, 0, i + 3, True)
            turn(NB - 1, 1, 0, False)
            either(3, last_w3)


def kernel(**inputs):
    import numpy as np
    import concourse.bacc as bacc
    from concourse.bass_utils import run_bass_kernel_spmd

    def get(name):
        return np.asarray(inputs["L0_" + name])

    x = get("attn_x").reshape(P, NB, TPB, E)
    arrays = {
        "xT": x.reshape(P, NB, TPB, EC, P).transpose(4, 1, 2, 3, 0).reshape(P, TOK * EC),
        "x_rows": x.reshape(P, NB * TPB * E),
        "wkv": np.concatenate([get("attn_wk"), get("attn_wv")], 0).T.reshape(EC, P, 2 * D).transpose(1, 0, 2),
        "wqT": np.concatenate([get("attn_wq")] * 2, 0).T.reshape(EC, P, 2 * D).transpose(1, 0, 2),
        "woT": get("attn_wo").T,
        "w1T": get("ffn_w1_w").T.reshape(EC, P, HID).transpose(1, 0, 2).reshape(P, EC * HID),
        "w2T": get("ffn_w2_w").T.reshape(EC, P, HID).transpose(1, 0, 2).reshape(P, EC * HID),
        "h1T": get("ffn_h1_w").T.reshape(HC, P, HID).transpose(1, 0, 2).reshape(P, HC * HID),
        "h2T": get("ffn_h2_w").T.reshape(HC, P, HID).transpose(1, 0, 2).reshape(P, HC * HID),
        "w3T": get("ffn_w3_w").T.reshape(HC, P, E).transpose(1, 0, 2).reshape(P, HC * E),
        "scales": np.stack([get("ffn_" + n).reshape(HC, P) for n in ("w1_s", "w2_s", "h1_s", "h2_s")]).transpose(2, 0, 1),
        "s3": get("ffn_w3_s"),
    }
    arrays = {n: np.ascontiguousarray(a) for n, a in arrays.items()}
    nc = bacc.Bacc("TRN2", target_bir_lowering=False, num_devices=1)
    args = [nc.dram_tensor("in_" + n, a.shape, mybir.dt.from_np(a.dtype), kind="ExternalInput").ap() for n, a in arrays.items()]
    out = nc.dram_tensor("out", (P, NB * TPB * E), mybir.dt.float32, kind="ExternalOutput").ap()
    build(nc, *args, out)
    r = run_bass_kernel_spmd(nc, [{"in_" + n: a for n, a in arrays.items()}], core_ids=[0])
    return r.results[0]["out"].reshape(1, TOK, E)
```
